# Optimizing a Trainium2 kernel written in Bass

```python
import numpy as np
import jax
import jax.numpy as jnp

def _softmax(x, axis=-1):
    return jax.nn.softmax(x, axis=axis)
def _gelu(x):
    return jax.nn.gelu(x, approximate=True)
def _silu(x):
    return jax.nn.silu(x)
def _sigmoid(x):
    return jax.nn.sigmoid(x)
def _layernorm(x, axis=-1, eps=1e-5):
    m = jnp.mean(x, axis=axis, keepdims=True)
    v = jnp.var(x, axis=axis, keepdims=True)
    return (x - m) / jnp.sqrt(v + eps)
def _scatter_add(tgt, idx, src, axis=0):
    return tgt.at[idx].add(src)
def _segment_sum(src, seg, n):
    return jax.ops.segment_sum(src, seg, n)

kernel_name = 'mk_adj_resnorm_d1_adj_64_a9d521'

def setup_inputs(seed: int = 0):
    np.random.seed(seed)
    _w = jnp.asarray
    def _rec_inputs():
        import jax
        import jax.numpy as jnp
        _gk = jax.random.key(seed)
        x = -9.806e-05 + 1 * jax.random.normal(jax.random.fold_in(_gk, 1), (8192, 64), jnp.float32)
        _a = jax.random.bernoulli(jax.random.fold_in(_gk, 2), 0.000976562, (8192, 8192))
        adj = _a.astype(jnp.int32)
        return x, adj
    x, adj = _rec_inputs()
    def _L0_gnn_setup():
        import jax, jax.numpy as jnp
        import numpy as np
        ALPHA = 0.2
        NEG_BIG = -9000000000000000.0
        key = jax.random.key(seed)
        k1, k2, k3, k4, k5 = jax.random.split(key, 5)
        N, M, F_in, F_out = (8192, 8192, 64, 64)
        item_embs = jax.random.normal(k1, (N, F_in), dtype=jnp.float32)
        entity_embs = jax.random.normal(k2, (M, F_in), dtype=jnp.float32)
        adj = jax.random.randint(k3, (N, M), 0, 2, dtype=jnp.int32)
        W = jax.random.normal(k4, (F_in, F_out), dtype=jnp.float32)
        a = jax.random.normal(k5, (2 * F_out, 1), dtype=jnp.float32)
        return {'item_embs': item_embs, 'entity_embs': entity_embs, 'adj': adj, 'W': W, 'a': a}
    _L0_gnn_all = _L0_gnn_setup()
    _L0_gnn_in = {k: v for k, v in _L0_gnn_all.items() if k in ('entity_embs', 'W', 'a', )}
    del _L0_gnn_all

    return {
        "x": x,
        "adj": adj,
        "L0_gnn_entity_embs": _L0_gnn_in["entity_embs"],
        "L0_gnn_W": _L0_gnn_in["W"],
        "L0_gnn_a": _L0_gnn_in["a"],
    }

def reference(x, adj, L0_gnn_entity_embs, L0_gnn_W, L0_gnn_a):
    import jax
    import jax.numpy as jnp
    def _L0_gnn_ref(item_embs, entity_embs, adj, W, a):
        import jax, jax.numpy as jnp
        import numpy as np
        ALPHA = 0.2
        NEG_BIG = -9000000000000000.0
        F_out = W.shape[1]
        Wh = item_embs @ W
        We = entity_embs @ W
        a1 = a[:F_out, 0]
        a2 = a[F_out:, 0]
        scores = (Wh @ a1)[:, None] + (We @ a2)[None, :]
        e = jnp.where(scores > 0, scores, ALPHA * scores)
        e = jnp.where(adj > 0, e, NEG_BIG)
        attention = jax.nn.softmax(e, axis=1)
        entity_emb_weighted = attention @ entity_embs
        h_prime = entity_emb_weighted + item_embs
        return jax.nn.elu(h_prime)

    x = _layernorm(x + _L0_gnn_ref(x, L0_gnn_entity_embs, adj, L0_gnn_W, L0_gnn_a), axis=-1)
    return x


_drawn_inputs = setup_inputs


def setup_inputs(seed=0):
    import zlib

    import numpy as np

    out = dict(_drawn_inputs(seed))
    spreads = {}
    factors = {}
    for name, (base, spread) in spreads.items():
        noise = np.random.default_rng([zlib.crc32(name.encode()), seed]).standard_normal(out[name].shape)
        drawn = base * np.exp(spread * noise) if base else spread * noise
        out[name] = jnp.asarray(drawn.astype(out[name].dtype))
    for name, factor in factors.items():
        out[name] = (out[name] * factor).astype(out[name].dtype)
    return out
```

```python
import concourse.bass as bass
from concourse import mybir
from contextlib import ExitStack


def gat_resnorm_kernel(
    nc: bass.Bass,
    x: bass.AP,
    adj: bass.AP,
    ent: bass.AP,
    w: bass.AP,
    a: bass.AP,
    v_row_dram: bass.AP,
    out: bass.AP,
):
    fp32 = mybir.dt.float32
    bf16 = mybir.dt.bfloat16
    ALU = mybir.AluOpType
    ACT = mybir.ActivationFunctionType
    AX = mybir.AxisListType

    P = 128
    N, F = x.shape
    M = ent.shape[0]
    SB = 512
    NB = SB // P
    NS = N // SB
    NT = M // P
    NPAIR = NT // 2
    HALF = M // 2
    NH = M // HALF
    QC = 1024
    QB = HALF // QC
    NQ = NH * NB * QB
    LEAD = 4
    ALPHA = 0.2
    BIG = 2.0 ** 53
    EPS = 1e-5
    CREDIT = 2

    x_rows = x.rearrange("(n p) f -> p n f", p=P)
    out_rows = out.rearrange("(n p) f -> p n f", p=P)
    adj_rows = adj.rearrange("(n p) m -> p n m", p=P)
    ent_tiles = ent.rearrange("(t p) f -> p t f", p=P)

    ctx = ExitStack()
    with ctx:
        def sb(name, shape, dt):
            return ctx.enter_context(nc.sbuf_tensor(name, shape, dt))

        def pb(name, shape, dt):
            return ctx.enter_context(nc.psum_tensor(name, shape, dt))

        def sem(name):
            return ctx.enter_context(nc.semaphore(name))

        marks = [sb(f"marks{i}", [P, NB, M], bf16) for i in range(2)]
        v_bcast = sb("v_bcast", [P, M], fp32)
        ent_sb = sb("ent_sb", [P, NT, F], fp32)
        expo = sb("expo", [P, 2, SB], fp32)
        probs = sb("probs", [P, 2, 2, SB], fp32)
        dsum = sb("dsum", [P, 2, SB], fp32)
        w8_bcast = sb("w8_bcast", [P, 2, SB], fp32)
        hsum = sb("hsum", [P, SB], fp32)
        w8_diag = hsum
        x_sb = sb("x_sb", [P, NB, F], fp32)
        y_a = sb("y_a", [P, NB, F], fp32)
        y_b = sb("y_b", [P, NB, F], fp32)
        d_rows = sb("d_rows", [P, 2, SB], bf16)
        ident_f = sb("ident_f", [P, P], fp32)
        ident_b = sb("ident_b", [P, P], bf16)
        neg_ident = sb("neg_ident", [P, P], bf16)
        ones_b = sb("ones_b", [P, P], bf16)
        ones_f = sb("ones_f", [P, P], fp32)
        fold = sb("fold", [P, F], fp32)
        v_col = sb("v_col", [P, NT], fp32)
        nv8_col = sb("nv8_col", [P, NT], fp32)
        w_col = sb("w_col", [P, N // P], fp32)
        mean_ent = sb("mean_ent", [P, 1, F], fp32)
        w_cur = sb("w_cur", [P, NB], fp32)
        w8_cur = sb("w8_cur", [P, NB], fp32)
        vmax_part = sb("vmax_part", [P, NB, NH * QB], fp32)
        g_a = sb("g_a", [P, NB], fp32)
        g_b = sb("g_b", [P, NB], fp32)
        g_c = sb("g_c", [P, NB], fp32)
        d_parts = sb("d_parts", [P, NB, 3], bf16)
        e_a = sb("e_a", [P, NB, 1], fp32)
        e_b = sb("e_b", [P, NB, 1], fp32)
        e_flag = sb("e_flag", [P, NB, 1], fp32)
        e_rstd = sb("e_rstd", [P, NB, 1], fp32)
        zero = sb("zero", [P, 1, 1], fp32)
        minus_half = sb("minus_half", [P, NB, 1], fp32)

        early = marks[1][:, :, :].rearrange("p b m -> p (b m)").bitcast(fp32)
        x_all = early[:, 0:N // P * F].rearrange("p (n f) -> p n f", f=F)
        prod = early[:, 4096:8192].rearrange("p (n f) -> p n f", f=F)
        w_in = early[0:F, 8192:8192 + F]
        wT = early[0:F, 8320:8320 + F]
        a_in = early[0:F, 8448:8450]
        a_wide = early[0:F, 8576:8576 + 2 * P].rearrange("p (c n) -> p c n", c=2)
        wa = early[:, 8960:8960 + 2 * F].rearrange("p (c o f) -> p c o f", c=2, o=1)
        v_rows = early[0:NT, 9216:9216 + P]
        mean_w = early[:, 9472:9472 + P]

        exp_ps = [pb(f"exp_ps{i}", [P, SB], fp32) for i in range(LEAD)]
        h_ps = pb("h_ps", [P, SB], fp32)
        epi_ps = pb("epi_ps", [P, NB, P], fp32)
        misc_ps = epi_ps[:, :, :].rearrange("p b f -> p (b f)")
        junk_ps = pb("junk_ps", [P, QC], fp32)

        adj_loaded = [[[sem(f"adj_loaded{i}{h}{b}") for b in range(NB)] for h in range(NH)] for i in range(2)]
        const_loaded = sem("const_loaded")
        x_all_loaded = sem("x_all_loaded")
        ent_loaded = sem("ent_loaded")
        v_stored = sem("v_stored")
        v_bcast_loaded = sem("v_bcast_loaded")
        pool_const = sem("pool_const")
        pro_dve = sem("pro_dve")
        pro_pe = sem("pro_pe")
        marked = sem("marked")
        maxed = sem("maxed")
        guard_step = sem("guard_step")
        d_rows_ps_ready = sem("d_rows_ps_ready")
        d_rows_ready = sem("d_rows_ready")
        w8_diag_ready = sem("w8_diag_ready")
        w8_ps_ready = sem("w8_ps_ready")
        w8_ready = sem("w8_ready")
        masked = sem("masked")
        expo_ready = sem("expo_ready")
        exp_done = sem("exp_done")
        summed = sem("summed")
        pv_done = sem("pv_done")
        h_copied = sem("h_copied")
        epi_ready = sem("epi_ready")
        epi_step = sem("epi_step")
        elu_exp = sem("elu_exp")
        rstd_ready = sem("rstd_ready")
        x_loaded = sem("x_loaded")
        out_stored = sem("out_stored")

        PRO_V, PRO_X, PRO_DVE = 8, 10, 13
        NGUARD = 11
        NEPI = 16

        def step_columns(q):
            h, r = divmod(q, NB * QB)
            b, k = divmod(r, QB)
            return h, b, h * QB + k

        MARK_AT = [int(1.7 * q) for q in range(NQ)]
        MAX_AT = [t + 2 for t in MARK_AT]
        GUARD_AT = NT - 7
        assert MAX_AT[-1] < GUARD_AT


        block = ctx.enter_context(nc.Block())

        @block.sync
        def _(sp):
            sp.dma_start(w_in, w).then_inc(const_loaded, 16)
            for c in range(2):
                sp.dma_start(a_in[:, c:c + 1], a[c * F:(c + 1) * F, :]).then_inc(const_loaded, 16)
            sp.dma_start(ent_sb[:, :, :], ent_tiles).then_inc(ent_loaded, 16)
            sp.dma_start(x_all, x_rows).then_inc(x_all_loaded, 16)
            sp.wait_ge(pro_dve, PRO_V)
            sp.dma_start(v_row_dram, v_rows).then_inc(v_stored, 16)
            sp.wait_ge(v_stored, 16)
            sp.dma_start(v_bcast[:, :], v_row_dram.rearrange("t p -> (t p)").partition_broadcast(P))\
              .then_inc(v_bcast_loaded, 16)

            sp.dma_start(x_sb[:, :, :], x_rows[:, 0:NB, :]).then_inc(x_loaded, 16)

            def store(s):
                sp.wait_ge(epi_step, (s + 1) * NEPI)
                sp.dma_start(out_rows[:, bass.ds(s * NB, NB), :], y_b[:, :, :]).then_inc(out_stored, 16)

            with sp.Fori(0, NS - 1) as s:
                store(s)
                sp.dma_start(x_sb[:, :, :], x_rows[:, bass.ds((s + 1) * NB, NB), :]).then_inc(x_loaded, 16)
            store(NS - 1)
            sp.wait_ge(out_stored, 16 * NS)

        @block.gpsimd
        def _(pool):
            def load(s, par, h):
                for b in range(NB):
                    pool.dma_start(marks[par][:, b, h * HALF:(h + 1) * HALF],
                                   adj_rows[:, bass.ds(s * NB + b, 1), h * HALF:(h + 1) * HALF]
                                   .rearrange("p o m -> p (o m)")).then_inc(adj_loaded[par][h][b], 16)

            load(0, 0, 0)
            load(0, 0, 1)
            pool.memset(ident_f[:, :], 0.0).then_inc(pool_const, 1)
            pool.wait_ge(pool_const, 1)
            pool.affine_select(out=ident_f[:, :], in_=ident_f[:, :], compare_op=ALU.not_equal, fill=1.0,
                               base=0, pattern=[[-1, P]], channel_multiplier=1).then_inc(pool_const, 1)
            pool.memset(ones_f[:, :], 1.0).then_inc(pool_const, 1)
            pool.memset(mean_w, 1.0 / M).then_inc(pool_const, 1)
            pool.memset(ones_b[:, :], 1.0).then_inc(pool_const, 1)
            pool.memset(minus_half[:, :, :], -0.5).then_inc(pool_const, 1)
            pool.memset(zero[:, :, :], 0.0).then_inc(pool_const, 1)
            pool.memset(d_rows[:, :, :], 0.0).then_inc(pool_const, 1)
            pool.wait_ge(pro_dve, PRO_DVE)
            pool.wait_ge(v_stored, 16)
            load(1, 1, 0)

            def period(s, par, last=False, load_next=True, load_after=True, first=False):
                for pair in range(NPAIR):
                    g = s * NPAIR + pair
                    pool.wait_ge(exp_done, (g + 1) * 2 + CREDIT)
                    if pair == 0:
                        if not first:
                            pool.wait_ge(epi_ready, s)
                        pool.tensor_tensor(dsum[:, :, :], probs[:, 0, :, :],
                                           zero[:, :, :].broadcast_to([P, 2, SB]), ALU.add).then_inc(summed, 1)
                    else:
                        pool.wait_ge(summed, g + CREDIT)
                        pool.tensor_tensor(dsum[:, :, :], dsum[:, :, :], probs[:, pair % 2, :, :],
                                           ALU.add).then_inc(summed, 1)
                    if pair == 1 and load_next:
                        if not first:
                            pool.wait_ge(masked, s * NT)
                        load(s + 1, 1 - par, 1)
                    if pair == 17 and load_after:
                        pool.wait_ge(masked, s * NT + NT // 2)
                        load(s + 2, par, 0)
                    if pair == 12 and not first:
                        pool.wait_ge(epi_step, (s - 1) * NEPI + NEPI - 1)
                        pool.tensor_tensor(e_rstd[:, :, :], e_a[:, :, :], minus_half[:, :, :],
                                           ALU.pow).then_inc(rstd_ready, 1)

            pool.sem_inc(summed, CREDIT)
            period(0, 0, first=True)
            with pool.Fori(0, (NS - 4) // 2) as k:
                period(k * 2 + 1, 1)
                period(k * 2 + 2, 0)
            period(NS - 3, 1)
            period(NS - 2, 0, load_after=False)
            period(NS - 1, 1, load_next=False, load_after=False)
            pool.wait_ge(epi_step, (NS - 1) * NEPI + NEPI - 1)
            pool.tensor_tensor(e_rstd[:, :, :], e_a[:, :, :], minus_half[:, :, :],
                               ALU.pow).then_inc(rstd_ready, 1)

        @block.scalar
        def _(act):
            def mark(s, par, q):
                h, b, c = step_columns(q)
                if q % QB == 0:
                    act.wait_ge(adj_loaded[par][h][b], load_count(s, par))
                piece = marks[par][:, b, c * QC:(c + 1) * QC]
                nc.scalar.activation(piece, piece, ACT.Relu, scale=-BIG, bias=BIG).then_inc(marked, 1)

            def load_count(s, par):
                return (s - par) * 8 + 16

            def copy_d_rows(s, par):
                act.wait_ge(d_rows_ps_ready, s + 1)
                nc.scalar.activation(d_rows[0:3, par, :], misc_ps[0:3, :], ACT.Copy).then_inc(d_rows_ready, 1)

            def diag_w8(s):
                act.wait_ge(guard_step, s * NGUARD + 6)
                for b in range(NB):
                    ins = nc.scalar.activation(w8_diag[:, b * P:(b + 1) * P], ident_f[:, :], ACT.Copy,
                                               scale=w8_cur[:, b:b + 1])
                ins.then_inc(w8_diag_ready, 1)

            def copy_w8(s, par):
                act.wait_ge(w8_ps_ready, s + 1)
                nc.scalar.activation(w8_bcast[:, par, :], misc_ps[:, :], ACT.Copy).then_inc(w8_ready, 1)

            def copy_h(s):
                act.wait_ge(pv_done, (s + 1) * NPAIR + CREDIT)
                nc.scalar.activation(hsum[:, :], h_ps[:, :], ACT.Copy).then_inc(h_copied, 1)

            def exp_of_h(s):
                act.wait_ge(epi_step, s * NEPI + 8)
                nc.scalar.activation(y_b[:, :, :], y_b[:, :, :], ACT.Exp).then_inc(elu_exp, 1)

            def period(s, par, last=False, first=False):
                for t in range(NT):
                    g = s * NT + t
                    act.wait_ge(expo_ready, g + 1)
                    if t % 2 == 0:
                        act.wait_ge(pv_done, s * NPAIR + t // 2 + 1)
                        act.wait_ge(summed, s * NPAIR + t // 2 + 1)
                    nc.scalar.activation(probs[:, t // 2 % 2, t % 2, :], expo[:, t % 2, :], ACT.Exp,
                                         bias=v_col[:, t:t + 1]).then_inc(exp_done, 1)
                    if t == 1 and not first:
                        copy_h(s - 1)
                    if t == 18 and not first:
                        exp_of_h(s - 1)
                    if not last:
                        if t in MARK_AT:
                            mark(s + 1, 1 - par, MARK_AT.index(t))
                        if t == GUARD_AT + 1:
                            copy_d_rows(s + 1, 1 - par)
                            diag_w8(s + 1)
                        if t == GUARD_AT + 3:
                            copy_w8(s + 1, 1 - par)

            act.sem_inc(exp_done, CREDIT)
            for q in range(NQ):
                mark(0, 0, q)
            act.wait_ge(pool_const, 8)
            copy_d_rows(0, 0)
            diag_w8(0)
            copy_w8(0, 0)
            period(0, 0, first=True)
            with act.Fori(0, (NS - 2) // 2) as k:
                period(k * 2 + 1, 1)
                period(k * 2 + 2, 0)
            period(NS - 1, 1, last=True)
            copy_h(NS - 1)
            exp_of_h(NS - 1)

        @block.vector
        def _(dve):
            def chained(ins, semaphore, count):
                ins.then_inc(semaphore, 1)
                dve.wait_ge(semaphore, count)

            dve.wait_ge(pool_const, 8)
            nc.vector.tensor_copy(ident_b[:, :], ident_f[:, :]).then_inc(pro_dve, 1)
            nc.vector.tensor_scalar(neg_ident[:, :], ident_f[:, :], -1.0, None, ALU.mult).then_inc(pro_dve, 1)
            dve.wait_ge(const_loaded, 48)
            for c in range(2):
                ins = nc.vector.tensor_scalar(a_wide[:, c, :], ones_f[0:F, :], a_in[:, c:c + 1], None, ALU.mult)
            ins.then_inc(pro_dve, 1)
            dve.wait_ge(pro_pe, 1)
            nc.vector.tensor_copy(wT, misc_ps[0:F, 0:F]).then_inc(pro_dve, 1)
            dve.wait_ge(pro_pe, 2)
            chained(nc.vector.tensor_copy(wa[:, :, 0, :],
                                          misc_ps[:, 128:128 + 2 * F].rearrange("p (c f) -> p c f", c=2)),
                    pro_dve, 5)
            dve.wait_ge(ent_loaded, 16)
            chained(nc.vector.tensor_tensor(prod, ent_sb[:, :, :], wa[:, 1, :, :].broadcast_to([P, NT, F]), ALU.mult),
                    pro_dve, 6)
            chained(nc.vector.tensor_reduce(v_col[:, :], prod, AX.X, ALU.add), pro_dve, 7)
            dve.wait_ge(pro_pe, 3)
            nc.vector.tensor_copy(v_rows, epi_ps[0:NT, 0, :]).then_inc(pro_dve, 1)
            dve.wait_ge(x_all_loaded, 16)
            chained(nc.vector.tensor_tensor(prod, x_all, wa[:, 0, :, :].broadcast_to([P, N // P, F]), ALU.mult),
                    pro_dve, PRO_V + 1)
            chained(nc.vector.tensor_reduce(w_col[:, :], prod, AX.X, ALU.add), pro_dve, PRO_X)
            nc.vector.tensor_scalar(nv8_col[:, :], v_col[:, :], -(1.0 - ALPHA), None, ALU.mult).then_inc(pro_dve, 1)
            nc.vector.tensor_tensor(fold[:, :], ident_f[:, 0:F], ident_f[:, F:2 * F], ALU.add).then_inc(pro_dve, 1)
            dve.wait_ge(pro_pe, 4)
            chained(nc.vector.tensor_copy(mean_ent[:, 0, :], epi_ps[:, 1, 0:F]), pro_dve, PRO_DVE)
            dve.wait_ge(v_bcast_loaded, 16)

            def row_max(s, par, q):
                _, b, c = step_columns(q)
                nc.vector.tensor_tensor_reduce(out=junk_ps[:, :], in0=v_bcast[:, c * QC:(c + 1) * QC],
                                               in1=marks[par][:, b, c * QC:(c + 1) * QC], scale=1.0,
                                               scalar=-3.0e38, op0=ALU.subtract, op1=ALU.max,
                                               accum_out=vmax_part[:, b, c:c + 1]).then_inc(maxed, 1)

            def guard(s):
                n = s * NGUARD
                dve.wait_ge(maxed, (s + 1) * NQ)
                nc.vector.tensor_reduce(g_a[:, :], vmax_part[:, :, :], AX.X, ALU.max).then_inc(guard_step, 1)
                chained(nc.vector.tensor_copy(w_cur[:, :], w_col[:, bass.ds(s * NB, NB)]), guard_step, n + 2)
                chained(nc.vector.tensor_tensor(g_b[:, :], g_a[:, :], w_cur[:, :], ALU.add), guard_step, n + 3)
                chained(nc.vector.scalar_tensor_tensor(out=g_a[:, :], in0=g_b[:, :], scalar=ALPHA, in1=g_b[:, :],
                                                       op0=ALU.mult, op1=ALU.max), guard_step, n + 4)
                chained(nc.vector.scalar_tensor_tensor(out=g_b[:, :], in0=w_cur[:, :], scalar=ALPHA, in1=g_a[:, :],
                                                       op0=ALU.mult, op1=ALU.subtract), guard_step, n + 5)
                chained(nc.vector.tensor_scalar(w8_cur[:, :], w_cur[:, :], 1.0 - ALPHA, None, ALU.mult),
                        guard_step, n + 6)
                chained(nc.vector.tensor_copy(d_parts[:, :, 0], g_b[:, :]), guard_step, n + 7)
                chained(nc.vector.tensor_tensor(g_a[:, :], g_b[:, :], d_parts[:, :, 0], ALU.subtract),
                        guard_step, n + 8)
                chained(nc.vector.tensor_copy(d_parts[:, :, 1], g_a[:, :]), guard_step, n + 9)
                chained(nc.vector.tensor_tensor(g_c[:, :], g_a[:, :], d_parts[:, :, 1], ALU.subtract),
                        guard_step, n + 10)
                chained(nc.vector.tensor_copy(d_parts[:, :, 2], g_c[:, :]), guard_step, n + 11)

            def wide(col):
                return col.broadcast_to([P, NB, F])

            def end_a(s):
                n = s * NEPI
                h, den = epi_ps[:, :, 0:F], epi_ps[:, :, F:F + 1]
                dve.wait_ge(epi_ready, s + 1)
                chained(nc.vector.tensor_scalar(e_flag[:, :, :], den, 0.0, None, ALU.is_equal), epi_step, n + 1)
                chained(nc.vector.tensor_tensor(e_a[:, :, :], den, e_flag[:, :, :], ALU.add), epi_step, n + 2)
                chained(nc.vector.reciprocal(e_b[:, :, :], e_a[:, :, :]), epi_step, n + 3)
                nc.vector.tensor_tensor(y_a[:, :, :], h, wide(e_b[:, :, :]), ALU.mult).then_inc(epi_step, 1)
                if not (isinstance(s, int) and s == 0):
                    dve.wait_ge(out_stored, s * 16)
                chained(nc.vector.tensor_tensor(y_b[:, :, :], mean_ent[:, :, :].broadcast_to([P, NB, F]),
                                                wide(e_flag[:, :, :]), ALU.mult), epi_step, n + 5)
                chained(nc.vector.tensor_tensor(y_a[:, :, :], y_a[:, :, :], y_b[:, :, :], ALU.add), epi_step, n + 6)
                dve.wait_ge(x_loaded, (s + 1) * 16)
                chained(nc.vector.tensor_tensor(y_a[:, :, :], y_a[:, :, :], x_sb[:, :, :], ALU.add), epi_step, n + 7)
                chained(nc.vector.tensor_scalar(y_b[:, :, :], y_a[:, :, :], 0.0, None, ALU.min), epi_step, n + 8)

            def end_b(s):
                n = s * NEPI
                dve.wait_ge(elu_exp, s + 1)
                chained(nc.vector.scalar_tensor_tensor(out=y_a[:, :, :], in0=y_a[:, :, :], scalar=0.0,
                                                       in1=y_b[:, :, :], op0=ALU.max, op1=ALU.add), epi_step, n + 9)
                chained(nc.vector.scalar_tensor_tensor(out=y_a[:, :, :], in0=y_a[:, :, :], scalar=-1.0,
                                                       in1=x_sb[:, :, :], op0=ALU.add, op1=ALU.add), epi_step, n + 10)
                chained(nc.vector.tensor_reduce(e_a[:, :, 0], y_a[:, :, :], AX.X, ALU.add), epi_step, n + 11)
                chained(nc.vector.scalar_tensor_tensor(out=y_a[:, :, :], in0=wide(e_a[:, :, :]), scalar=-1.0 / F,
                                                       in1=y_a[:, :, :], op0=ALU.mult, op1=ALU.add), epi_step, n + 12)
                chained(nc.vector.tensor_tensor(y_b[:, :, :], y_a[:, :, :], y_a[:, :, :], ALU.mult), epi_step, n + 13)
                chained(nc.vector.tensor_reduce(e_b[:, :, 0], y_b[:, :, :], AX.X, ALU.add), epi_step, n + 14)
                chained(nc.vector.tensor_scalar(e_a[:, :, :], e_b[:, :, :], 1.0 / F, EPS, ALU.mult, ALU.add),
                        epi_step, n + 15)

            def end_c(s):
                n = s * NEPI
                dve.wait_ge(rstd_ready, s + 1)
                nc.vector.tensor_tensor(y_b[:, :, :], y_a[:, :, :], wide(e_rstd[:, :, :]), ALU.mult)\
                    .then_inc(epi_step, 1)

            def period(s, par, last=False, first=False):
                for t in range(NT):
                    g = s * NT + t
                    if t == 0:
                        dve.wait_ge(w8_ready, s + 1)
                    if not last and t in MAX_AT:
                        dve.wait_ge(marked, (s + 1) * NQ + MAX_AT.index(t) + 1)
                        dve.wait_ge(maxed, (s + 1) * NQ + MAX_AT.index(t))
                    dve.wait_ge(masked, g + 1)
                    dve.wait_ge(exp_done, g + 1)
                    nc.vector.scalar_tensor_tensor(out=expo[:, t % 2, :], in0=w8_bcast[:, par, :],
                                                   scalar=nv8_col[:, t:t + 1], in1=exp_ps[t % LEAD][:, :],
                                                   op0=ALU.max, op1=ALU.add).then_inc(expo_ready, 1)
                    if not last and t in MAX_AT:
                        row_max(s + 1, 1 - par, MAX_AT.index(t))
                    if not first:
                        if t == 12:
                            end_a(s - 1)
                        if t == 20:
                            end_b(s - 1)
                        if t == 28:
                            end_c(s - 1)
                    if not last and t == GUARD_AT:
                        guard(s + 1)

            for q in range(NQ):
                dve.wait_ge(marked, q + 1)
                if q:
                    dve.wait_ge(maxed, q)
                row_max(0, 0, q)
            guard(0)
            period(0, 0, first=True)
            with dve.Fori(0, (NS - 2) // 2) as k:
                period(k * 2 + 1, 1)
                period(k * 2 + 2, 0)
            period(NS - 1, 1, last=True)
            end_a(NS - 1)
            end_b(NS - 1)
            end_c(NS - 1)

        @block.tensor
        def _(pe):
            pe.wait_ge(pool_const, 8)
            pe.wait_ge(const_loaded, 48)
            nc.tensor.matmul(misc_ps[0:F, 0:F], w_in, ident_f[0:F, 0:F], start=True, stop=True).then_inc(pro_pe, 1)
            pe.wait_ge(pro_dve, 4)
            for c in range(2):
                mm = nc.tensor.matmul(misc_ps[:, 128 + c * F:128 + (c + 1) * F], a_wide[:, c, :], wT,
                                      start=True, stop=True)
            mm.then_inc(pro_pe, 1)
            pe.wait_ge(pro_dve, 7)
            nc.tensor.matmul(epi_ps[0:NT, 0, :], v_col[:, :], ident_f[:, :], start=True, stop=True)\
                .then_inc(pro_pe, 1)
            pe.wait_ge(pro_dve, PRO_V)
            for t in range(NT):
                mm = nc.tensor.matmul(epi_ps[:, 1, 0:F], mean_w, ent_sb[:, t, :], start=(t == 0), stop=(t == NT - 1))
            mm.then_inc(pro_pe, 1)

            def mask(s, par, t, wait=True):
                if wait:
                    pe.wait_ge(expo_ready, s * NT + t - LEAD + 1)
                if t == 0:
                    pe.wait_ge(d_rows_ready, s + 1)
                bank = exp_ps[t % LEAD]
                nc.tensor.matmul(bank[:, :], ones_b[:, :], d_rows[:, par, :], start=True, stop=True,
                                 skip_group_check=True)
                for b in range(NB):
                    mm = nc.tensor.matmul(bank[:, b * P:(b + 1) * P], marks[par][:, b, t * P:(t + 1) * P],
                                          neg_ident[:, :], start=False, stop=True,
                                          skip_group_check=True)
                mm.then_inc(masked, 1)

            def weighted(s, pair):
                pe.wait_ge(exp_done, (s * NPAIR + pair + 1) * 2 + CREDIT)
                for i in range(2):
                    mm = nc.tensor.matmul(h_ps[i * F:(i + 1) * F, :], ent_sb[:, 2 * pair + i, :],
                                          probs[:, pair % 2, i, :], start=(pair == 0), stop=(pair == NPAIR - 1),
                                          skip_group_check=True)
                mm.then_inc(pv_done, 1)

            def guard_rows(s):
                pe.wait_ge(guard_step, s * NGUARD + 11)
                if not (isinstance(s, int) and s == 0):
                    pe.wait_ge(w8_ready, s)
                for b in range(NB):
                    mm = nc.tensor.matmul(misc_ps[0:3, b * P:(b + 1) * P], d_parts[:, b, :], ident_b[:, :],
                                          start=True, stop=True)
                mm.then_inc(d_rows_ps_ready, 1)

            def guard_w8(s):
                pe.wait_ge(d_rows_ready, s + 1)
                pe.wait_ge(w8_diag_ready, s + 1)
                nc.tensor.matmul(misc_ps[:, :], ones_f[:, :], w8_diag[:, :], start=True, stop=True)\
                    .then_inc(w8_ps_ready, 1)

            def turn(s):
                pe.wait_ge(h_copied, s + 1)
                pe.wait_ge(summed, (s + 1) * NPAIR + CREDIT)
                if not (isinstance(s, int) and s == 0):
                    pe.wait_ge(epi_step, s * NEPI)
                for b in range(NB):
                    nc.tensor.matmul(epi_ps[:, b, 0:F], hsum[:, b * P:(b + 1) * P], fold[:, :],
                                     start=True, stop=True)
                    for i in range(2):
                        mm = nc.tensor.matmul(epi_ps[:, b, F:F + 1], dsum[:, i, b * P:(b + 1) * P],
                                              ones_f[:, 0:1], start=(i == 0), stop=(i == 1))
                mm.then_inc(epi_ready, 1)

            def period(s, par, last=False, first=False):
                for t in range(NT):
                    if t + LEAD < NT:
                        mask(s, par, t + LEAD)
                    elif not last:
                        mask(s + 1, 1 - par, t + LEAD - NT)
                    if t % 2 == 1:
                        if t == 1 and not first:
                            pe.wait_ge(h_copied, s)
                        weighted(s, t // 2)
                    if t == 2 and not first:
                        turn(s - 1)
                    if not last and t == GUARD_AT + 1:
                        guard_rows(s + 1)
                    if not last and t == GUARD_AT + 2:
                        guard_w8(s + 1)

            pe.sem_inc(pv_done, CREDIT)
            pe.wait_ge(pro_dve, PRO_DVE)
            guard_rows(0)
            guard_w8(0)
            for t in range(LEAD):
                mask(0, 0, t, wait=False)
            period(0, 0, first=True)
            with pe.Fori(0, (NS - 2) // 2) as k:
                period(k * 2 + 1, 1)
                period(k * 2 + 2, 0)
            period(NS - 1, 1, last=True)
            turn(NS - 1)


_INS = ["x", "adj", "L0_gnn_entity_embs", "L0_gnn_W", "L0_gnn_a"]


def kernel(**inputs):
    import numpy as _np
    import concourse.bacc as _bacc
    from concourse import mybir as _mybir
    from concourse.bass_utils import run_bass_kernel_spmd as _run

    nc = _bacc.Bacc("TRN2", target_bir_lowering=False, num_devices=1)
    arrays, args = {}, []
    for name in _INS:
        a = _np.ascontiguousarray(inputs[name])
        arrays[f"in_{name}_dram"] = a
        args.append(nc.dram_tensor(f"in_{name}_dram", a.shape, _mybir.dt.from_np(a.dtype), kind="ExternalInput").ap())
    entities = inputs["L0_gnn_entity_embs"].shape[0]
    scratch = nc.dram_tensor("v_row_dram", (entities // 128, 128), _mybir.dt.float32, kind="Internal").ap()
    shape = tuple(inputs["x"].shape)
    out = nc.dram_tensor("out_0_dram", shape, _mybir.dt.float32, kind="ExternalOutput").ap()
    gat_resnorm_kernel(nc, *args, scratch, out)
    r = _run(nc, [arrays], core_ids=[0])
    return r.results[0]["out_0_dram"]
```

```python
import concourse.bass as bass
from concourse import mybir
from contextlib import ExitStack


def gat_resnorm_kernel(
    nc: bass.Bass,
    x: bass.AP,
    adj: bass.AP,
    ent: bass.AP,
    w: bass.AP,
    a: bass.AP,
    out: bass.AP,
):
    fp32 = mybir.dt.float32
    bf16 = mybir.dt.bfloat16
    ALU = mybir.AluOpType
    ACT = mybir.ActivationFunctionType
    AX = mybir.AxisListType

    P = 128
    N, F = x.shape
    M = ent.shape[0]
    SB = 512
    NB = SB // P
    NS = N // SB
    NT = M // P
    NPAIR = NT // 2
    NC = 4
    QC = M // NC
    CT = QC // P
    LH = 2
    LB = NB // LH
    SLOTS = 6
    TURN = 3
    assert TURN * NC % SLOTS == 0 and NS % TURN == 1
    NQ = NC * NB
    G = 32
    LEAD = 4
    ALPHA = 0.2
    BIG = 2.0 ** 53
    EPS = 1e-5
    CREDIT = 4
    NX = 8
    XP, XO = 8, 6
    NXT = NT // XP
    ND = NT - NXT
    RELU_AHEAD, ADD_AHEAD = 4, 1
    FREE = NX + 1
    assert ND % NX == 0 and ND % LEAD == 0
    GP = 3
    NGP = NPAIR // CREDIT * GP

    x_rows = x.rearrange("(n p) f -> p n f", p=P)
    out_rows = out.rearrange("(n p) f -> p n f", p=P)
    adj_rows = adj.rearrange("(n p) m -> p n m", p=P)
    ent_tiles = ent.rearrange("(t p) f -> p t f", p=P)

    ctx = ExitStack()
    with ctx:
        def sb(name, shape, dt):
            return ctx.enter_context(nc.sbuf_tensor(name, shape, dt))

        def pb(name, shape, dt):
            return ctx.enter_context(nc.psum_tensor(name, shape, dt))

        def sem(name):
            return ctx.enter_context(nc.semaphore(name))

        marks = [sb(f"marks{i}", [P, NB, QC], bf16) for i in range(SLOTS)]
        v_bcast = sb("v_bcast", [P, M], fp32)
        ent_sb = sb("ent_sb", [P, NT, F], fp32)
        expo = sb("expo", [P, NX, SB], fp32)
        relu_x = sb("relu_x", [P, SB], fp32)
        probs = sb("probs", [P, CREDIT, 2, SB], fp32)
        dsum = sb("dsum", [P, 2, SB], fp32)
        w8_bcast = sb("w8_bcast", [P, TURN, SB], fp32)
        hsum = sb("hsum", [P, SB], fp32)
        w8_diag = hsum
        x_sb = sb("x_sb", [P, NB, F], fp32)
        y_a = sb("y_a", [P, NB, F], fp32)
        y_b = sb("y_b", [P, NB, F], fp32)
        d_rows = sb("d_rows", [P, TURN, SB], bf16)
        ident_f = sb("ident_f", [P, P], fp32)
        ident_b = sb("ident_b", [P, P], bf16)
        neg_ident = sb("neg_ident", [P, P], bf16)
        ones_b = sb("ones_b", [P, P], bf16)
        den_sb = sb("den_sb", [2 * G, SB], fp32)
        per_g = sb("per_g", [2 * G, 1], fp32)
        ones_f = sb("ones_f", [P, P], fp32)
        fold = sb("fold", [P, F], fp32)
        v_col = sb("v_col", [P, NT], fp32)
        nv8_col = sb("nv8_col", [P, NT], fp32)
        v8_col = sb("v8_col", [P, NT], fp32)
        v2_col = sb("v2_col", [P, NT], fp32)
        w_col = sb("w_col", [P, N // P], fp32)
        mean_ent = sb("mean_ent", [P, 1, F], fp32)
        w_cur = sb("w_cur", [P, NB], fp32)
        w8_cur = sb("w8_cur", [P, NB], fp32)
        vmax_part = sb("vmax_part", [P, TURN, NB, NC], fp32)
        junk = sb("junk", [P, QC], bf16)
        g_a = sb("g_a", [P, NB], fp32)
        g_b = sb("g_b", [P, NB], fp32)
        g_c = sb("g_c", [P, NB], fp32)
        d_parts = sb("d_parts", [P, NB, 3], bf16)
        e_a = sb("e_a", [P, NB, 1], fp32)
        e_b = sb("e_b", [P, NB, 1], fp32)
        e_flag = sb("e_flag", [P, NB, 1], fp32)
        e_rstd = sb("e_rstd", [P, NB, 1], fp32)
        zero = sb("zero", [P, 1, 1], fp32)
        minus_half = sb("minus_half", [P, NB, 1], fp32)

        x_all = probs[:, :, :, :].rearrange("p a b n -> p (a b n)").rearrange("p (n f) -> p n f", f=F)
        prod = marks[4][:, :, :].rearrange("p b m -> p (b m)").bitcast(fp32).rearrange("p (n f) -> p n f", f=F)
        early = marks[5][:, :, :].rearrange("p b m -> p (b m)").bitcast(fp32)
        w_in = early[0:F, 0:F]
        wT = early[0:F, 64:64 + F]
        a_in = early[0:F, 128:130]
        a_wide = early[0:F, 256:256 + 2 * P].rearrange("p (c n) -> p c n", c=2)
        wa = early[:, 512:512 + 2 * F].rearrange("p (c o f) -> p c o f", c=2, o=1)
        v_rows = early[0:NT, 768:768 + P]
        mean_w = early[:, 1024:1024 + P]

        exp_ps = [pb(f"exp_ps{i}", [P, SB], fp32) for i in range(LEAD)]
        exp_x_ps = pb("exp_x_ps", [P, SB], fp32)
        h_ps = pb("h_ps", [P, SB], fp32)
        epi_ps = pb("epi_ps", [P, NB, P], fp32)
        den_ps = pb("den_ps", [P, SB], fp32)
        misc_ps = epi_ps[:, :, :].rearrange("p b f -> p (b f)")

        adj_loaded = [[sem(f"adj_loaded{i}{h}") for h in range(LH)] for i in range(SLOTS)]
        const_loaded = sem("const_loaded")
        x_all_loaded = sem("x_all_loaded")
        ent_loaded = sem("ent_loaded")
        v_bcast_ps_ready = sem("v_bcast_ps_ready")
        v_bcast_ready = sem("v_bcast_ready")
        x_prod = sem("x_prod")
        pool_const = sem("pool_const")
        pro_dve = sem("pro_dve")
        pro_pe = sem("pro_pe")
        marked = sem("marked")
        maxed = sem("maxed")
        guard_step = sem("guard_step")
        d_rows_ps_ready = sem("d_rows_ps_ready")
        d_rows_ready = sem("d_rows_ready")
        w8_diag_ready = sem("w8_diag_ready")
        w8_ps_ready = sem("w8_ps_ready")
        w8_ready = sem("w8_ready")
        masked = sem("masked")
        expo_ready = sem("expo_ready")
        relu_ready = sem("relu_ready")
        x_exp_ready = sem("x_exp_ready")
        exp_done = sem("exp_done")
        summed = sem("summed")
        pv_done = sem("pv_done")
        h_copied = sem("h_copied")
        epi_ready = sem("epi_ready")
        epi_step = sem("epi_step")
        elu_exp = sem("elu_exp")
        rstd_ready = sem("rstd_ready")
        x_loaded = sem("x_loaded")
        out_stored = sem("out_stored")

        PRO_WA, PRO_V, PRO_ROWS, PRO_DVE = 5, 7, 8, 12
        NGUARD = 11
        NEPI = 16

        def slot(ph, c):
            return (ph * NC + c) % SLOTS

        def loads_of_slot(k, ph, c):
            return k * (TURN * NC // SLOTS) + (ph * NC + c) // SLOTS + 1

        STEP = NT // NQ
        MARK_AHEAD, MAX_AHEAD = 3, 1
        MARK_T, MAX_T = 1, 0
        GUARD_AT = (NQ - MAX_AHEAD - 1) * STEP + MAX_T + 1

        def step(s, k, ph, n):
            if isinstance(s, int) and (s + 1) * NQ + n >= NS * NQ:
                return None
            k, ph = after(k, ph)
            if n >= NQ:
                k, ph = after(k, ph)
            return k, ph, n % NQ

        def without_dve(t):
            return t % XP == XO

        def dve_tile(t):
            return t - (t + XP - 1 - XO) // XP

        def back(t, n):
            d = 0
            while n:
                d += 1
                n -= not without_dve(t - d)
            return d

        def pair_of_gpsimd(pair):
            return pair // CREDIT * GP + min(pair % CREDIT, GP)

        def after(k, ph):
            return (k + (ph + 1) // TURN, (ph + 1) % TURN)

        def superblocks(eng, period):
            period(0, 0, 0, first=True)
            with eng.Fori(0, (NS - 1 - TURN) // TURN) as k:
                for ph in range(1, TURN + 1):
                    period(k * TURN + ph, *after(k, ph - 1))
            for s in range(NS - TURN, NS):
                period(s, s // TURN, s % TURN, last=(s == NS - 1))

        block = ctx.enter_context(nc.Block())

        @block.sync
        def _(sp):
            sp.dma_start(w_in, w).then_inc(const_loaded, 16)
            for c in range(2):
                sp.dma_start(a_in[:, c:c + 1], a[c * F:(c + 1) * F, :]).then_inc(const_loaded, 16)
            sp.dma_start(ent_sb[:, :, :], ent_tiles).then_inc(ent_loaded, 16)
            sp.dma_start(x_all, x_rows).then_inc(x_all_loaded, 16)
            sp.dma_start(x_sb[:, :, :], x_rows[:, 0:NB, :]).then_inc(x_loaded, 16)

            def store(s):
                sp.wait_ge(epi_step, (s + 1) * NEPI)
                sp.dma_start(out_rows[:, bass.ds(s * NB, NB), :], y_b[:, :, :]).then_inc(out_stored, 16)

            with sp.Fori(0, NS - 1) as s:
                store(s)
                sp.dma_start(x_sb[:, :, :], x_rows[:, bass.ds((s + 1) * NB, NB), :]).then_inc(x_loaded, 16)
            store(NS - 1)
            sp.wait_ge(out_stored, 16 * NS)

        @block.gpsimd
        def _(pool):
            def load(s, ph, c):
                for h in range(LH):
                    pool.dma_start(marks[slot(ph, c)][:, h * LB:(h + 1) * LB, :],
                                   adj_rows[:, bass.ds(s * NB + h * LB, LB), c * QC:(c + 1) * QC])\
                        .then_inc(adj_loaded[slot(ph, c)][h], 16)

            pool.memset(ident_f[:, :], 0.0).then_inc(pool_const, 1)
            pool.wait_ge(pool_const, 1)
            pool.affine_select(out=ident_f[:, :], in_=ident_f[:, :], compare_op=ALU.not_equal, fill=1.0,
                               base=0, pattern=[[-1, P]], channel_multiplier=1).then_inc(pool_const, 1)
            pool.memset(ones_f[:, :], 1.0).then_inc(pool_const, 1)
            pool.memset(mean_w, 1.0 / M).then_inc(pool_const, 1)
            pool.memset(ones_b[:, :], 1.0).then_inc(pool_const, 1)
            pool.memset(minus_half[:, :, :], -0.5).then_inc(pool_const, 1)
            pool.memset(per_g[:, :], 1.0 / G).then_inc(pool_const, 1)
            pool.memset(zero[:, :, :], 0.0).then_inc(pool_const, 1)
            pool.memset(d_rows[:, :, :], 0.0).then_inc(pool_const, 1)
            pool.wait_ge(ent_loaded, 16)
            for c in range(NC):
                load(0, 0, c)
            pool.wait_ge(pro_dve, PRO_WA)
            pool.wait_ge(x_all_loaded, 16)
            pool.tensor_tensor(x_all, x_all, wa[:, 0, :, :].broadcast_to([P, N // P, F]), ALU.mult)\
                .then_inc(x_prod, 1)
            pool.wait_ge(pro_dve, PRO_V)
            load(1, 1, 0)
            pool.wait_ge(pro_dve, PRO_DVE)
            pool.wait_ge(pro_pe, 4)
            load(1, 1, 1)

            def period(s, k, ph, first=False, last=False):
                _, ph1 = after(k, ph)
                _, ph2 = after(k, ph1)
                for pair in range(NPAIR):
                    if pair % CREDIT < GP:
                        n = s * NGP + pair_of_gpsimd(pair)
                        pool.wait_ge(exp_done, (s * NPAIR + pair + 1) * 2 + FREE)
                        if pair == 0:
                            if not first:
                                pool.wait_ge(epi_ready, s)
                            pool.tensor_tensor(dsum[:, :, :], probs[:, 0, :, :],
                                               zero[:, :, :].broadcast_to([P, 2, SB]), ALU.add)\
                                .then_inc(summed, 1)
                        else:
                            pool.wait_ge(summed, n + GP)
                            pool.tensor_tensor(dsum[:, :, :], dsum[:, :, :], probs[:, pair % CREDIT, :, :],
                                               ALU.add).then_inc(summed, 1)
                    if pair == 6 and not last:
                        pool.wait_ge(masked, s * NT + CT)
                        load(s + 1, ph1, 2)
                    if pair == 14 and not last:
                        pool.wait_ge(masked, s * NT + 2 * CT)
                        load(s + 1, ph1, 3)
                    if pair == 22 and not last and not (isinstance(s, int) and s == NS - 2):
                        pool.wait_ge(masked, s * NT + 3 * CT)
                        load(s + 2, ph2, 0)
                    if pair == 30 and not last and not (isinstance(s, int) and s == NS - 2):
                        pool.wait_ge(masked, s * NT + 4 * CT)
                        load(s + 2, ph2, 1)
                    if pair == 12 and not first:
                        pool.wait_ge(epi_step, (s - 1) * NEPI + NEPI - 1)
                        pool.tensor_tensor(e_rstd[:, :, :], e_a[:, :, :], minus_half[:, :, :],
                                           ALU.pow).then_inc(rstd_ready, 1)

            pool.sem_inc(summed, GP)
            superblocks(pool, period)
            pool.wait_ge(epi_step, (NS - 1) * NEPI + NEPI - 1)
            pool.tensor_tensor(e_rstd[:, :, :], e_a[:, :, :], minus_half[:, :, :],
                               ALU.pow).then_inc(rstd_ready, 1)

        @block.scalar
        def _(act):
            def mark(k, ph, q):
                c, b = divmod(q, NB)
                if b % LB == 0:
                    act.wait_ge(adj_loaded[slot(ph, c)][b // LB], loads_of_slot(k, ph, c) * 16)
                piece = marks[slot(ph, c)][:, b, :]
                nc.scalar.activation(piece, piece, ACT.Relu, scale=-BIG, bias=BIG).then_inc(marked, 1)

            def copy_d_rows(s, ph):
                act.wait_ge(d_rows_ps_ready, s + 1)
                nc.scalar.activation(d_rows[0:3, ph, :], misc_ps[0:3, :], ACT.Copy).then_inc(d_rows_ready, 1)

            def diag_w8(s):
                act.wait_ge(guard_step, s * NGUARD + 6)
                for b in range(NB):
                    ins = nc.scalar.activation(w8_diag[:, b * P:(b + 1) * P], ident_f[:, :], ACT.Copy,
                                               scale=w8_cur[:, b:b + 1])
                ins.then_inc(w8_diag_ready, 1)

            def copy_w8(s, ph):
                act.wait_ge(w8_ps_ready, s + 1)
                nc.scalar.activation(w8_bcast[:, ph, :], misc_ps[:, :], ACT.Copy).then_inc(w8_ready, 1)

            def copy_h(s):
                act.wait_ge(pv_done, (s + 1) * NPAIR + CREDIT)
                nc.scalar.activation(den_sb[:, :], den_ps[0:2 * G, :], ACT.Copy)
                nc.scalar.activation(hsum[:, :], h_ps[:, :], ACT.Copy).then_inc(h_copied, 1)

            def exp_of_h(s):
                act.wait_ge(epi_step, s * NEPI + 8)
                nc.scalar.activation(y_b[:, :, :], y_b[:, :, :], ACT.Exp).then_inc(elu_exp, 1)

            def period(s, k, ph, first=False, last=False):
                k1, ph1 = after(k, ph)
                for t in range(NT):
                    g = s * NT + t
                    if without_dve(t):
                        act.wait_ge(x_exp_ready, s * NXT + t // XP + 1)
                        exponents, bias = exp_x_ps[:, :], v2_col
                    else:
                        act.wait_ge(expo_ready, s * ND + dve_tile(t) + 1)
                        exponents, bias = expo[:, dve_tile(t) % NX, :], v_col
                    if t % 2 == 0:
                        act.wait_ge(pv_done, s * NPAIR + t // 2 + 1)
                        if t // 2 % CREDIT < GP:
                            act.wait_ge(summed, s * NGP + pair_of_gpsimd(t // 2) + 1)
                    nc.scalar.activation(probs[:, t // 2 % CREDIT, t % 2, :], exponents, ACT.Exp,
                                         bias=bias[:, t:t + 1]).then_inc(exp_done, 1)
                    if t == 2 and not first:
                        copy_h(s - 1)
                    if t == 18 and not first:
                        exp_of_h(s - 1)
                    if without_dve(t + RELU_AHEAD) and t + RELU_AHEAD < NT:
                        nc.scalar.activation(relu_x[:, :], w8_bcast[:, ph, :], ACT.Relu,
                                             bias=v8_col[:, t + RELU_AHEAD:t + RELU_AHEAD + 1])\
                            .then_inc(relu_ready, 1)
                    if t % STEP == MARK_T and step(s, k, ph, MARK_AHEAD + t // STEP):
                        mark(*step(s, k, ph, MARK_AHEAD + t // STEP))
                    if not last:
                        if t == GUARD_AT + 1:
                            copy_d_rows(s + 1, ph1)
                            diag_w8(s + 1)
                        if t == GUARD_AT + 3:
                            copy_w8(s + 1, ph1)

            act.sem_inc(exp_done, FREE)
            for c in range(NC):
                for q in range(c * NB, (c + 1) * NB):
                    mark(0, 0, q)
                for m in range(c * NB, (c + 1) * NB):
                    act.wait_ge(v_bcast_ps_ready, m + 1)
                    nc.scalar.activation(v_bcast[:, m * SB:(m + 1) * SB], exp_ps[m % LEAD][:, :], ACT.Copy)\
                        .then_inc(v_bcast_ready, 1)
            act.wait_ge(pool_const, 9)
            copy_d_rows(0, 0)
            diag_w8(0)
            copy_w8(0, 0)
            for q in range(MARK_AHEAD):
                mark(0, 1, q)
            superblocks(act, period)
            copy_h(NS - 1)
            exp_of_h(NS - 1)

        @block.vector
        def _(dve):
            def chained(ins, semaphore, count):
                ins.then_inc(semaphore, 1)
                dve.wait_ge(semaphore, count)

            dve.wait_ge(pool_const, 9)
            nc.vector.tensor_copy(ident_b[:, :], ident_f[:, :]).then_inc(pro_dve, 1)
            nc.vector.tensor_scalar(neg_ident[:, :], ident_f[:, :], -1.0, None, ALU.mult).then_inc(pro_dve, 1)
            dve.wait_ge(const_loaded, 48)
            for c in range(2):
                ins = nc.vector.tensor_scalar(a_wide[:, c, :], ones_f[0:F, :], a_in[:, c:c + 1], None, ALU.mult)
            ins.then_inc(pro_dve, 1)
            dve.wait_ge(pro_pe, 1)
            nc.vector.tensor_copy(wT, misc_ps[0:F, 0:F]).then_inc(pro_dve, 1)
            dve.wait_ge(pro_pe, 2)
            chained(nc.vector.tensor_copy(wa[:, :, 0, :],
                                          misc_ps[:, 128:128 + 2 * F].rearrange("p (c f) -> p c f", c=2)),
                    pro_dve, 5)
            dve.wait_ge(ent_loaded, 16)
            chained(nc.vector.tensor_tensor(prod, ent_sb[:, :, :], wa[:, 1, :, :].broadcast_to([P, NT, F]), ALU.mult),
                    pro_dve, 6)
            chained(nc.vector.tensor_reduce(v_col[:, :], prod, AX.X, ALU.add), pro_dve, 7)
            dve.wait_ge(pro_pe, 3)
            nc.vector.tensor_copy(v_rows, epi_ps[0:NT, 0, :]).then_inc(pro_dve, 1)
            nc.vector.tensor_scalar(v8_col[:, :], v_col[:, :], 1.0 - ALPHA, None, ALU.mult)
            nc.vector.tensor_scalar(v2_col[:, :], v_col[:, :], ALPHA, None, ALU.mult)
            nc.vector.tensor_scalar(nv8_col[:, :], v_col[:, :], -(1.0 - ALPHA), None, ALU.mult).then_inc(pro_dve, 1)
            nc.vector.tensor_tensor(fold[:, :], ident_f[:, 0:F], ident_f[:, F:2 * F], ALU.add).then_inc(pro_dve, 1)

            def w_and_mean():
                dve.wait_ge(x_prod, 1)
                nc.vector.tensor_reduce(w_col[:, :], x_all, AX.X, ALU.add).then_inc(pro_dve, 1)
                dve.wait_ge(pro_pe, 4)
                chained(nc.vector.tensor_copy(mean_ent[:, 0, :], epi_ps[:, 1, 0:F]), pro_dve, PRO_DVE)

            def row_max(ph, q):
                c, b = divmod(q, NB)
                nc.vector.tensor_tensor_reduce(out=junk[:, :], in0=v_bcast[:, c * QC:(c + 1) * QC],
                                               in1=marks[slot(ph, c)][:, b, :], scale=1.0,
                                               scalar=-3.0e38, op0=ALU.subtract, op1=ALU.max,
                                               accum_out=vmax_part[:, ph, b, c:c + 1]).then_inc(maxed, 1)

            def guard(s, ph):
                n = s * NGUARD
                dve.wait_ge(maxed, (s + 1) * NQ)
                nc.vector.tensor_reduce(g_a[:, :], vmax_part[:, ph, :, :], AX.X, ALU.max).then_inc(guard_step, 1)
                chained(nc.vector.tensor_copy(w_cur[:, :], w_col[:, bass.ds(s * NB, NB)]), guard_step, n + 2)
                chained(nc.vector.tensor_tensor(g_b[:, :], g_a[:, :], w_cur[:, :], ALU.add), guard_step, n + 3)
                chained(nc.vector.scalar_tensor_tensor(out=g_a[:, :], in0=g_b[:, :], scalar=ALPHA, in1=g_b[:, :],
                                                       op0=ALU.mult, op1=ALU.max), guard_step, n + 4)
                chained(nc.vector.scalar_tensor_tensor(out=g_b[:, :], in0=w_cur[:, :], scalar=ALPHA, in1=g_a[:, :],
                                                       op0=ALU.mult, op1=ALU.subtract), guard_step, n + 5)
                chained(nc.vector.tensor_scalar(w8_cur[:, :], w_cur[:, :], 1.0 - ALPHA, None, ALU.mult),
                        guard_step, n + 6)
                chained(nc.vector.tensor_copy(d_parts[:, :, 0], g_b[:, :]), guard_step, n + 7)
                chained(nc.vector.tensor_tensor(g_a[:, :], g_b[:, :], d_parts[:, :, 0], ALU.subtract),
                        guard_step, n + 8)
                chained(nc.vector.tensor_copy(d_parts[:, :, 1], g_a[:, :]), guard_step, n + 9)
                chained(nc.vector.tensor_tensor(g_c[:, :], g_a[:, :], d_parts[:, :, 1], ALU.subtract),
                        guard_step, n + 10)
                chained(nc.vector.tensor_copy(d_parts[:, :, 2], g_c[:, :]), guard_step, n + 11)

            def wide(col):
                return col.broadcast_to([P, NB, F])

            def end_a(s):
                n = s * NEPI
                h, den = epi_ps[:, :, 0:F], epi_ps[:, :, F:F + 1]
                dve.wait_ge(epi_ready, s + 1)
                chained(nc.vector.tensor_scalar(e_flag[:, :, :], den, 0.0, None, ALU.is_equal), epi_step, n + 1)
                chained(nc.vector.tensor_tensor(e_a[:, :, :], den, e_flag[:, :, :], ALU.add), epi_step, n + 2)
                chained(nc.vector.reciprocal(e_b[:, :, :], e_a[:, :, :]), epi_step, n + 3)
                nc.vector.tensor_tensor(y_a[:, :, :], h, wide(e_b[:, :, :]), ALU.mult).then_inc(epi_step, 1)
                if not (isinstance(s, int) and s == 0):
                    dve.wait_ge(out_stored, s * 16)
                chained(nc.vector.tensor_tensor(y_b[:, :, :], mean_ent[:, :, :].broadcast_to([P, NB, F]),
                                                wide(e_flag[:, :, :]), ALU.mult), epi_step, n + 5)
                chained(nc.vector.tensor_tensor(y_a[:, :, :], y_a[:, :, :], y_b[:, :, :], ALU.add), epi_step, n + 6)
                dve.wait_ge(x_loaded, (s + 1) * 16)
                chained(nc.vector.tensor_tensor(y_a[:, :, :], y_a[:, :, :], x_sb[:, :, :], ALU.add), epi_step, n + 7)
                chained(nc.vector.tensor_scalar(y_b[:, :, :], y_a[:, :, :], 0.0, None, ALU.min), epi_step, n + 8)

            def end_b(s):
                n = s * NEPI
                dve.wait_ge(elu_exp, s + 1)
                chained(nc.vector.scalar_tensor_tensor(out=y_a[:, :, :], in0=y_a[:, :, :], scalar=0.0,
                                                       in1=y_b[:, :, :], op0=ALU.max, op1=ALU.add), epi_step, n + 9)
                chained(nc.vector.scalar_tensor_tensor(out=y_a[:, :, :], in0=y_a[:, :, :], scalar=-1.0,
                                                       in1=x_sb[:, :, :], op0=ALU.add, op1=ALU.add), epi_step, n + 10)
                chained(nc.vector.tensor_reduce(e_a[:, :, 0], y_a[:, :, :], AX.X, ALU.add), epi_step, n + 11)
                chained(nc.vector.scalar_tensor_tensor(out=y_a[:, :, :], in0=wide(e_a[:, :, :]), scalar=-1.0 / F,
                                                       in1=y_a[:, :, :], op0=ALU.mult, op1=ALU.add), epi_step, n + 12)
                chained(nc.vector.tensor_tensor(y_b[:, :, :], y_a[:, :, :], y_a[:, :, :], ALU.mult), epi_step, n + 13)
                chained(nc.vector.tensor_reduce(e_b[:, :, 0], y_b[:, :, :], AX.X, ALU.add), epi_step, n + 14)
                chained(nc.vector.tensor_scalar(e_a[:, :, :], e_b[:, :, :], 1.0 / F, EPS, ALU.mult, ALU.add),
                        epi_step, n + 15)

            def end_c(s):
                n = s * NEPI
                dve.wait_ge(rstd_ready, s + 1)
                nc.vector.tensor_tensor(y_b[:, :, :], y_a[:, :, :], wide(e_rstd[:, :, :]), ALU.mult)\
                    .then_inc(epi_step, 1)

            def period(s, k, ph, first=False, last=False):
                k1, ph1 = after(k, ph)
                for t in range(NT):
                    g = s * NT + t
                    if t == 0:
                        dve.wait_ge(w8_ready, s + 1)
                    n = MAX_AHEAD + t // STEP
                    maximum = step(s, k, ph, n) if t % STEP == MAX_T else None
                    if maximum:
                        dve.wait_ge(marked, (s + 1) * NQ + n + 1)
                        dve.wait_ge(maxed, (s + 1) * NQ + n)
                    if not without_dve(t):
                        dve.wait_ge(masked, g + 1)
                        dve.wait_ge(exp_done, g - back(t, NX) + 1 + FREE)
                        nc.vector.scalar_tensor_tensor(out=expo[:, dve_tile(t) % NX, :], in0=w8_bcast[:, ph, :],
                                                       scalar=nv8_col[:, t:t + 1],
                                                       in1=exp_ps[dve_tile(t) % LEAD][:, :],
                                                       op0=ALU.max, op1=ALU.add).then_inc(expo_ready, 1)
                    if maximum:
                        row_max(*maximum[1:])
                    if not first:
                        if t == 12:
                            end_a(s - 1)
                        if t == 20:
                            end_b(s - 1)
                        if t == 28:
                            end_c(s - 1)
                    if not last and t == GUARD_AT:
                        guard(s + 1, ph1)

            for n in range(NQ + MAX_AHEAD):
                if n % NB == 0 and n < NQ:
                    dve.wait_ge(v_bcast_ready, n + NB)
                dve.wait_ge(marked, n + 1)
                if n:
                    dve.wait_ge(maxed, n)
                row_max(n // NQ, n % NQ)
                if n == NQ - NB:
                    w_and_mean()
                if n == NQ - 1:
                    guard(0, 0)
            superblocks(dve, period)
            end_a(NS - 1)
            end_b(NS - 1)
            end_c(NS - 1)

        @block.tensor
        def _(pe):
            pe.wait_ge(pool_const, 9)
            pe.wait_ge(const_loaded, 48)
            nc.tensor.matmul(misc_ps[0:F, 0:F], w_in, ident_f[0:F, 0:F], start=True, stop=True).then_inc(pro_pe, 1)
            pe.wait_ge(pro_dve, 4)
            for c in range(2):
                mm = nc.tensor.matmul(misc_ps[:, 128 + c * F:128 + (c + 1) * F], a_wide[:, c, :], wT,
                                      start=True, stop=True)
            mm.then_inc(pro_pe, 1)
            pe.wait_ge(pro_dve, 7)
            nc.tensor.matmul(epi_ps[0:NT, 0, :], v_col[:, :], ident_f[:, :], start=True, stop=True)\
                .then_inc(pro_pe, 1)
            pe.wait_ge(pro_dve, PRO_ROWS)
            for t in range(NT):
                m = t // NB
                if t % NB == 0 and m >= LEAD:
                    pe.wait_ge(v_bcast_ready, m - LEAD + 1)
                mm = nc.tensor.matmul(exp_ps[m % LEAD][:, t % NB * P:(t % NB + 1) * P],
                                      ident_f[0:NT, t:t + 1].broadcast_to([NT, P]), v_rows,
                                      start=True, stop=True)
                if t % NB == NB - 1:
                    mm.then_inc(v_bcast_ps_ready, 1)
            for t in range(NT):
                mm = nc.tensor.matmul(epi_ps[:, 1, 0:F], mean_w, ent_sb[:, t, :], start=(t == 0), stop=(t == NT - 1))
            mm.then_inc(pro_pe, 1)

            def mask(s, ph, t, wait=True):
                if without_dve(t):
                    if wait and not (isinstance(s, int) and s == 0 and t < XP):
                        pe.wait_ge(exp_done, s * NT + t - XP + 1 + FREE)
                elif wait:
                    pe.wait_ge(expo_ready, s * ND + dve_tile(t) - LEAD + 1)
                if t == 0:
                    pe.wait_ge(d_rows_ready, s + 1)
                bank = exp_x_ps if without_dve(t) else exp_ps[dve_tile(t) % LEAD]
                nc.tensor.matmul(bank[:, :], ones_b[:, :], d_rows[:, ph, :], start=True, stop=True,
                                 skip_group_check=True)
                for b in range(NB):
                    mm = nc.tensor.matmul(bank[:, b * P:(b + 1) * P], marks[slot(ph, t // CT)][:, b, t % CT * P:(t % CT + 1) * P],
                                          neg_ident[:, :], start=False, stop=True,
                                          skip_group_check=True)
                mm.then_inc(masked, 1)

            def add_relu(s, t):
                pe.wait_ge(relu_ready, s * NXT + t // XP + 1)
                nc.tensor.matmul(exp_x_ps[:, :], ident_f[:, :], relu_x[:, :], start=False, stop=True,
                                 skip_group_check=True).then_inc(x_exp_ready, 1)

            def weighted(s, pair):
                pe.wait_ge(exp_done, (s * NPAIR + pair + 1) * 2 + FREE)
                for i in range(2):
                    mm = nc.tensor.matmul(h_ps[i * F:(i + 1) * F, :], ent_sb[:, 2 * pair + i, :],
                                          probs[:, pair % CREDIT, i, :], start=(pair == 0), stop=(pair == NPAIR - 1),
                                          skip_group_check=True)
                if pair % CREDIT >= GP:
                    for i in range(2):
                        mm = nc.tensor.matmul(den_ps[i * G:(i + 1) * G, :], ones_f[:, 0:G],
                                              probs[:, pair % CREDIT, i, :], start=(pair == GP),
                                              stop=(pair == NPAIR - 1), skip_group_check=True)
                mm.then_inc(pv_done, 1)

            def guard_rows(s):
                pe.wait_ge(guard_step, s * NGUARD + 11)
                if not (isinstance(s, int) and s == 0):
                    pe.wait_ge(w8_ready, s)
                for b in range(NB):
                    mm = nc.tensor.matmul(misc_ps[0:3, b * P:(b + 1) * P], d_parts[:, b, :], ident_b[:, :],
                                          start=True, stop=True)
                mm.then_inc(d_rows_ps_ready, 1)

            def guard_w8(s):
                pe.wait_ge(d_rows_ready, s + 1)
                pe.wait_ge(w8_diag_ready, s + 1)
                nc.tensor.matmul(misc_ps[:, :], ones_f[:, :], w8_diag[:, :], start=True, stop=True)\
                    .then_inc(w8_ps_ready, 1)

            def turn(s):
                pe.wait_ge(h_copied, s + 1)
                pe.wait_ge(summed, (s + 1) * NGP + GP)
                if not (isinstance(s, int) and s == 0):
                    pe.wait_ge(epi_step, s * NEPI)
                for b in range(NB):
                    nc.tensor.matmul(epi_ps[:, b, 0:F], hsum[:, b * P:(b + 1) * P], fold[:, :],
                                     start=True, stop=True)
                    for i in range(2):
                        nc.tensor.matmul(epi_ps[:, b, F:F + 1], dsum[:, i, b * P:(b + 1) * P],
                                              ones_f[:, 0:1], start=(i == 0), stop=False)
                    mm = nc.tensor.matmul(epi_ps[:, b, F:F + 1], den_sb[:, b * P:(b + 1) * P], per_g[:, :],
                                          start=False, stop=True)
                mm.then_inc(epi_ready, 1)

            def period(s, k, ph, first=False, last=False):
                k1, ph1 = after(k, ph)
                for t in range(NT):
                    if t + LEAD < NT:
                        mask(s, ph, t + LEAD)
                    elif not last:
                        mask(s + 1, ph1, t + LEAD - NT)
                    if t == 1 and not first:
                        weighted(s - 1, NPAIR - 1)
                    if t % 2 == 1 and t > 1:
                        if t == 3 and not first:
                            pe.wait_ge(h_copied, s)
                        weighted(s, t // 2 - 1)
                    if without_dve(t + ADD_AHEAD) and t + ADD_AHEAD < NT:
                        add_relu(s, t + ADD_AHEAD)
                    if t == 5 and not first:
                        turn(s - 1)
                    if not last and t == GUARD_AT + 1:
                        guard_rows(s + 1)
                    if not last and t == GUARD_AT + 2:
                        guard_w8(s + 1)

            pe.sem_inc(pv_done, CREDIT)
            pe.wait_ge(pro_dve, PRO_DVE)
            guard_rows(0)
            guard_w8(0)
            pe.wait_ge(v_bcast_ready, NT // NB)
            for t in range(LEAD):
                mask(0, 0, t, wait=False)
            superblocks(pe, period)
            weighted(NS - 1, NPAIR - 1)
            turn(NS - 1)


_INS = ["x", "adj", "L0_gnn_entity_embs", "L0_gnn_W", "L0_gnn_a"]


def kernel(**inputs):
    import numpy as _np
    import concourse.bacc as _bacc
    from concourse import mybir as _mybir
    from concourse.bass_utils import run_bass_kernel_spmd as _run

    nc = _bacc.Bacc("TRN2", target_bir_lowering=False, num_devices=1)
    arrays, args = {}, []
    for name in _INS:
        a = _np.ascontiguousarray(inputs[name])
        arrays[f"in_{name}_dram"] = a
        args.append(nc.dram_tensor(f"in_{name}_dram", a.shape, _mybir.dt.from_np(a.dtype), kind="ExternalInput").ap())
    shape = tuple(inputs["x"].shape)
    out = nc.dram_tensor("out_0_dram", shape, _mybir.dt.float32, kind="ExternalOutput").ap()
    gat_resnorm_kernel(nc, *args, out)
    r = _run(nc, [arrays], core_ids=[0])
    return r.results[0]["out_0_dram"]
```

```python
import concourse.bass as bass
from concourse import mybir
from contextlib import ExitStack


def gat_resnorm_kernel(
    nc: bass.Bass,
    x: bass.AP,
    adj: bass.AP,
    ent: bass.AP,
    w: bass.AP,
    a: bass.AP,
    out: bass.AP,
):
    fp32 = mybir.dt.float32
    bf16 = mybir.dt.bfloat16
    ALU = mybir.AluOpType
    ACT = mybir.ActivationFunctionType
    AX = mybir.AxisListType

    P = 128
    N, F = x.shape
    M = ent.shape[0]
    SB = 512
    NB = SB // P
    NS = N // SB
    NT = M // P
    NPAIR = NT // 2
    NC = 4
    QC = M // NC
    CT = QC // P
    LH = 2
    LB = NB // LH
    SLOTS = 6
    TURN = 3
    assert TURN * NC % SLOTS == 0 and NS % TURN == 1
    NQ = NC * NB
    G = 32
    LEAD = 4
    ALPHA = 0.2
    BIG = 2.0 ** 53
    EPS = 1e-5
    CREDIT = 4
    NX = 8
    XP, XO = 8, 6
    NXT = NT // XP
    ND = NT - NXT
    RELU_AHEAD, ADD_AHEAD = 6, 1
    EARLY_MARKS = 2
    X_AFTER = 2
    DIAG_AT = 27
    TURN_AT = 6, 7, 8, 9
    FREE = NX + 1
    assert ND % NX == 0 and ND % LEAD == 0
    GP = 3
    NGP = NPAIR // CREDIT * GP

    x_rows = x.rearrange("(n p) f -> p n f", p=P)
    out_rows = out.rearrange("(n p) f -> p n f", p=P)
    adj_rows = adj.rearrange("(n p) m -> p n m", p=P)
    ent_tiles = ent.rearrange("(t p) f -> p t f", p=P)

    ctx = ExitStack()
    with ctx:
        def sb(name, shape, dt):
            return ctx.enter_context(nc.sbuf_tensor(name, shape, dt))

        def pb(name, shape, dt):
            return ctx.enter_context(nc.psum_tensor(name, shape, dt))

        def sem(name):
            return ctx.enter_context(nc.semaphore(name))

        marks = [sb(f"marks{i}", [P, NB, QC], bf16) for i in range(SLOTS)]
        v_bcast = sb("v_bcast", [P, M], fp32)
        ent_sb = sb("ent_sb", [P, NT, F], fp32)
        expo = sb("expo", [P, NX, SB], fp32)
        relu_x = sb("relu_x", [P, SB], fp32)
        probs = sb("probs", [P, CREDIT, 2, SB], fp32)
        dsum = sb("dsum", [P, 2, SB], fp32)
        w8_bcast = sb("w8_bcast", [P, TURN, SB], fp32)
        hsum = sb("hsum", [P, SB], fp32)
        w8_diag = hsum
        x_sb = sb("x_sb", [P, NB, F], fp32)
        y_a = sb("y_a", [P, NB, F], fp32)
        y_b = sb("y_b", [P, NB, F], fp32)
        y_c = sb("y_c", [P, NB, F], fp32)
        d_rows = sb("d_rows", [P, TURN, SB], bf16)
        ident_f = sb("ident_f", [P, P], fp32)
        ident_b = sb("ident_b", [P, P], bf16)
        neg_ident = sb("neg_ident", [P, P], bf16)
        ones_b = sb("ones_b", [P, P], bf16)
        den_sb = sb("den_sb", [2 * G, SB], fp32)
        per_g = sb("per_g", [2 * G, 1], fp32)
        ones_f = sb("ones_f", [P, P], fp32)
        fold = sb("fold", [P, F], fp32)
        v_col = sb("v_col", [P, NT], fp32)
        nv8_col = sb("nv8_col", [P, NT], fp32)
        v8_col = sb("v8_col", [P, NT], fp32)
        v2_col = sb("v2_col", [P, NT], fp32)
        w_col = sb("w_col", [P, N // P], fp32)
        mean_ent = sb("mean_ent", [P, 1, F], fp32)
        w_cur = sb("w_cur", [P, NB], fp32)
        w8_cur = sb("w8_cur", [P, NB, 1], fp32)
        vmax_part = sb("vmax_part", [P, TURN, NB, NC], fp32)
        junk = sb("junk", [P, QC], bf16)
        g_a = sb("g_a", [P, NB], fp32)
        g_b = sb("g_b", [P, NB], fp32)
        g_c = sb("g_c", [P, NB], fp32)
        d_parts = sb("d_parts", [P, NB, 3], bf16)
        e_a = sb("e_a", [P, NB, 1], fp32)
        e_b = sb("e_b", [P, NB, 1], fp32)
        e_flag = sb("e_flag", [P, NB, 1], fp32)
        e_rstd = sb("e_rstd", [P, NB, 1], fp32)
        minus_one = sb("minus_one", [P, 1, 1], fp32)
        minus_half = sb("minus_half", [P, NB, 1], fp32)

        x_all = probs[:, :, :, :].rearrange("p a b n -> p (a b n)").rearrange("p (n f) -> p n f", f=F)
        prod = marks[4][:, :, :].rearrange("p b m -> p (b m)").bitcast(fp32).rearrange("p (n f) -> p n f", f=F)
        early = marks[5][:, :, :].rearrange("p b m -> p (b m)").bitcast(fp32)
        w_in = early[0:F, 0:F]
        wT = early[0:F, 64:64 + F]
        a_in = early[0:F, 128:130]
        a_wide = early[0:F, 256:256 + 2 * P].rearrange("p (c n) -> p c n", c=2)
        wa = early[:, 512:512 + 2 * F].rearrange("p (c o f) -> p c o f", c=2, o=1)
        v_rows = early[:, 768:768 + NC * P].rearrange("p (c n) -> p c n", c=NC)
        mean_w = early[:, 1280:1280 + P]
        early_junk = [junk[:, :], expo[:, 0:2, :].rearrange("p a n -> p (a n)").bitcast(bf16)]

        exp_ps = [pb(f"exp_ps{i}", [P, SB], fp32) for i in range(LEAD)]
        exp_x_ps = pb("exp_x_ps", [P, SB], fp32)
        h_ps = pb("h_ps", [P, SB], fp32)
        epi_ps = pb("epi_ps", [P, NB, P], fp32)
        den_ps = pb("den_ps", [P, SB], fp32)
        misc_ps = epi_ps[:, :, :].rearrange("p b f -> p (b f)")

        adj_loaded = [[sem(f"adj_loaded{i}{h}") for h in range(LH)] for i in range(SLOTS)]
        const_loaded = sem("const_loaded")
        x_all_loaded = sem("x_all_loaded")
        ent_loaded = [sem(f"ent_loaded{c}") for c in range(NC)]
        v_step = sem("v_step")
        v_turned = sem("v_turned")
        v_rows_ready = sem("v_rows_ready")
        v_bcast_ps_ready = sem("v_bcast_ps_ready")
        v_bcast_ready = sem("v_bcast_ready")
        x_prod = sem("x_prod")
        pool_const = sem("pool_const")
        pro_dve = sem("pro_dve")
        pro_pe = sem("pro_pe")
        marked = sem("marked")
        maxed = sem("maxed")
        guard_step = sem("guard_step")
        d_rows_ps_ready = sem("d_rows_ps_ready")
        d_rows_ready = sem("d_rows_ready")
        w8_diag_ready = sem("w8_diag_ready")
        w8_ps_ready = sem("w8_ps_ready")
        w8_ready = sem("w8_ready")
        masked = sem("masked")
        expo_ready = sem("expo_ready")
        relu_ready = sem("relu_ready")
        x_exp_ready = sem("x_exp_ready")
        exp_done = sem("exp_done")
        summed = sem("summed")
        pv_done = sem("pv_done")
        h_copied = sem("h_copied")
        sums_folded = sem("sums_folded")
        epi_ready = sem("epi_ready")
        epi_step = sem("epi_step")
        elu_exp = sem("elu_exp")
        pool_epi_step = sem("pool_epi_step")
        x_loaded = sem("x_loaded")
        out_stored = sem("out_stored")

        PRO_WA, PRO_DVE = 5, 9
        NGUARD = 11
        NEPI = 8
        NPOOL, POOL_H, POOL_SUM, POOL_SQUARE = 11, 3, 7, 9
        DIVIDE_AT, MEAN_AT, VARIANCE_AT = 13, 32, 48
        EXP_AT = 22
        H_AT, SUM_AT, CENTRE_AT, NORM_AT = 8, 12, 18, 24

        def slot(ph, c):
            return (ph * NC + c) % SLOTS

        def loads_of_slot(k, ph, c):
            return k * (TURN * NC // SLOTS) + (ph * NC + c) // SLOTS + 1

        STEP = NT // NQ
        MARK_AHEAD, MAX_AHEAD = 3, 1
        MARK_T, MAX_T = 1, 0
        GUARD_AT = (NQ - MAX_AHEAD - 1) * STEP + MAX_T + 1

        def step(s, k, ph, n):
            if isinstance(s, int) and (s + 1) * NQ + n >= NS * NQ:
                return None
            k, ph = after(k, ph)
            if n >= NQ:
                k, ph = after(k, ph)
            return k, ph, n % NQ

        def without_dve(t, last=False):
            return t % XP == XO and not (last and t >= 0)

        def dve_tile(t, last=False):
            return t if last else t - (t + XP - 1 - XO) // XP

        def back(t, n, last):
            d = 0
            while n:
                d += 1
                n -= not without_dve(t - d, last)
            return d

        def pair_of_gpsimd(pair):
            return pair // CREDIT * GP + min(pair % CREDIT, GP)

        def after(k, ph):
            return (k + (ph + 1) // TURN, (ph + 1) % TURN)

        def superblocks(eng, period):
            period(0, 0, 0, first=True)
            with eng.Fori(0, (NS - 1 - TURN) // TURN) as k:
                for ph in range(1, TURN + 1):
                    period(k * TURN + ph, *after(k, ph - 1))
            for s in range(NS - TURN, NS):
                period(s, s // TURN, s % TURN, last=(s == NS - 1))

        block = ctx.enter_context(nc.Block())

        @block.sync
        def _(sp):
            sp.dma_start(w_in, w).then_inc(const_loaded, 16)
            for c in range(2):
                sp.dma_start(a_in[:, c:c + 1], a[c * F:(c + 1) * F, :]).then_inc(const_loaded, 16)
            for c in range(NC):
                sp.dma_start(ent_sb[:, c * CT:(c + 1) * CT, :], ent_tiles[:, c * CT:(c + 1) * CT, :])\
                    .then_inc(ent_loaded[c], 16)
            sp.wait_ge(adj_loaded[slot(0, 0)][0], 16)
            sp.dma_start(x_all, x_rows).then_inc(x_all_loaded, 16)
            sp.dma_start(x_sb[:, :, :], x_rows[:, 0:NB, :]).then_inc(x_loaded, 16)

            def store(s):
                sp.wait_ge(pool_epi_step, (s + 1) * NPOOL)
                sp.dma_start(out_rows[:, bass.ds(s * NB, NB), :], y_b[:, :, :]).then_inc(out_stored, 16)

            with sp.Fori(0, NS - 1) as s:
                store(s)
                sp.dma_start(x_sb[:, :, :], x_rows[:, bass.ds((s + 1) * NB, NB), :]).then_inc(x_loaded, 16)
            store(NS - 1)
            sp.wait_ge(out_stored, 16 * NS)

        @block.gpsimd
        def _(pool):
            def load(s, ph, c):
                for h in range(LH):
                    pool.dma_start(marks[slot(ph, c)][:, h * LB:(h + 1) * LB, :],
                                   adj_rows[:, bass.ds(s * NB + h * LB, LB), c * QC:(c + 1) * QC])\
                        .then_inc(adj_loaded[slot(ph, c)][h], 16)

            pool.memset(ident_f[:, :], 0.0).then_inc(pool_const, 1)
            pool.wait_ge(pool_const, 1)
            pool.affine_select(out=ident_f[:, :], in_=ident_f[:, :], compare_op=ALU.not_equal, fill=1.0,
                               base=0, pattern=[[-1, P]], channel_multiplier=1).then_inc(pool_const, 1)
            pool.memset(ones_f[:, :], 1.0).then_inc(pool_const, 1)
            pool.memset(mean_w, 1.0 / M).then_inc(pool_const, 1)
            pool.memset(ones_b[:, :], 1.0).then_inc(pool_const, 1)
            pool.memset(minus_half[:, :, :], -0.5).then_inc(pool_const, 1)
            pool.memset(per_g[:, :], 1.0 / G).then_inc(pool_const, 1)
            pool.memset(v_rows, 0.0).then_inc(pool_const, 1)
            pool.memset(minus_one[:, :, :], -1.0).then_inc(pool_const, 1)
            pool.memset(d_rows[:, :, :], 0.0).then_inc(pool_const, 1)
            pool.wait_ge(ent_loaded[NC - 2], 16)
            for c in range(NC):
                if c == X_AFTER:
                    pool.wait_ge(adj_loaded[slot(0, 0)][LH - 1], 16)
                load(0, 0, c)
            pool.wait_ge(v_step, 2 * NC)
            load(1, 1, 0)
            pool.wait_ge(pro_dve, PRO_WA)
            pool.wait_ge(x_all_loaded, 16)
            pool.tensor_tensor(x_all, x_all, wa[:, 0, :, :].broadcast_to([P, N // P, F]), ALU.mult)\
                .then_inc(x_prod, 1)
            pool.wait_ge(x_prod, 1)
            pool.tensor_tensor(x_all[:, :, 0:F // 2], x_all[:, :, 0:F // 2], x_all[:, :, F // 2:F], ALU.add)\
                .then_inc(x_prod, 1)
            pool.wait_ge(pro_pe, 3)
            load(1, 1, 1)

            def chained(ins, count):
                ins.then_inc(pool_epi_step, 1)
                pool.wait_ge(pool_epi_step, count)

            def diag_w8(s):
                pool.wait_ge(guard_step, s * NGUARD + 6)
                if not (isinstance(s, int) and s <= 1):
                    pool.wait_ge(epi_ready, (s - 1) * NB)
                pool.tensor_tensor(w8_diag[:, :].rearrange("p (b n) -> p b n", b=NB),
                                   ident_f[:, :].rearrange("p (o n) -> p o n", o=1).broadcast_to([P, NB, P]),
                                   w8_cur[:, :, :].broadcast_to([P, NB, P]), ALU.mult).then_inc(w8_diag_ready, 1)

            def rows_of(col):
                return col.broadcast_to([P, NB, F])

            def h_and_x(s):
                n = s * NPOOL
                pool.wait_ge(epi_step, s * NEPI + 4)
                if not (isinstance(s, int) and s == 0):
                    pool.wait_ge(out_stored, s * 16)
                chained(pool.tensor_tensor(y_b[:, :, :], mean_ent[:, :, :].broadcast_to([P, NB, F]),
                                           rows_of(e_flag[:, :, :]), ALU.mult), n + 1)
                chained(pool.tensor_tensor(y_a[:, :, :], y_a[:, :, :], y_b[:, :, :], ALU.add), n + 2)
                pool.wait_ge(x_loaded, (s + 1) * 16)
                pool.tensor_tensor(y_a[:, :, :], y_a[:, :, :], x_sb[:, :, :], ALU.add).then_inc(pool_epi_step, 1)

            def elu_and_x(s):
                n = s * NPOOL
                pool.wait_ge(elu_exp, (s + 1) * 2)
                chained(pool.tensor_tensor(y_a[:, :, :], y_a[:, :, :], y_b[:, :, :], ALU.add), n + 4)
                chained(pool.tensor_tensor(y_a[:, :, :], y_a[:, :, :], y_c[:, :, :], ALU.add), n + 5)
                chained(pool.tensor_tensor(y_a[:, :, :], y_a[:, :, :], minus_one[:, :, :].broadcast_to([P, NB, F]),
                                           ALU.add), n + 6)
                pool.tensor_tensor(y_a[:, :, :], y_a[:, :, :], x_sb[:, :, :], ALU.add).then_inc(pool_epi_step, 1)

            def centre(s):
                n = s * NPOOL
                pool.wait_ge(epi_step, s * NEPI + 6)
                chained(pool.tensor_tensor(y_a[:, :, :], y_a[:, :, :], rows_of(e_b[:, :, :]), ALU.add), n + 8)
                pool.tensor_tensor(y_b[:, :, :], y_a[:, :, :], y_a[:, :, :], ALU.mult).then_inc(pool_epi_step, 1)

            def normalise(s):
                n = s * NPOOL
                pool.wait_ge(epi_step, (s + 1) * NEPI)
                chained(pool.tensor_tensor(e_rstd[:, :, :], e_a[:, :, :], minus_half[:, :, :], ALU.pow), n + 10)
                pool.tensor_tensor(y_b[:, :, :], y_a[:, :, :], rows_of(e_rstd[:, :, :]), ALU.mult)\
                    .then_inc(pool_epi_step, 1)

            def period(s, k, ph, first=False, last=False):
                _, ph1 = after(k, ph)
                _, ph2 = after(k, ph1)
                for pair in range(NPAIR):
                    if pair == 6 and not last:
                        pool.wait_ge(masked, s * NT + CT)
                        load(s + 1, ph1, 2)
                    if pair == 14 and not last:
                        pool.wait_ge(masked, s * NT + 2 * CT)
                        load(s + 1, ph1, 3)
                    if pair == 22 and not last and not (isinstance(s, int) and s == NS - 2):
                        pool.wait_ge(masked, s * NT + 3 * CT)
                        load(s + 2, ph2, 0)
                    if pair == 30 and not last and not (isinstance(s, int) and s == NS - 2):
                        pool.wait_ge(masked, s * NT + 4 * CT)
                        load(s + 2, ph2, 1)
                    if pair % CREDIT < GP and pair > 0:
                        n = s * NGP + pair_of_gpsimd(pair)
                        pool.wait_ge(exp_done, (s * NPAIR + pair + 1) * 2 + FREE)
                        if pair == 1:
                            if not first:
                                pool.wait_ge(sums_folded, s)
                            pool.tensor_tensor(dsum[:, :, :], probs[:, 0, :, :], probs[:, 1, :, :], ALU.add)\
                                .then_inc(summed, 2)
                        else:
                            pool.wait_ge(summed, n + GP)
                            pool.tensor_tensor(dsum[:, :, :], dsum[:, :, :], probs[:, pair % CREDIT, :, :],
                                               ALU.add).then_inc(summed, 1)
                    if not last and pair == DIAG_AT:
                        diag_w8(s + 1)
                    if not first:
                        if pair == H_AT:
                            h_and_x(s - 1)
                        if pair == SUM_AT:
                            elu_and_x(s - 1)
                        if pair == CENTRE_AT:
                            centre(s - 1)
                        if pair == NORM_AT:
                            normalise(s - 1)

            pool.sem_inc(summed, GP)
            diag_w8(0)
            superblocks(pool, period)
            h_and_x(NS - 1)
            elu_and_x(NS - 1)
            centre(NS - 1)
            normalise(NS - 1)

        @block.scalar
        def _(act):
            def mark(k, ph, q):
                c, b = divmod(q, NB)
                if b % LB == 0:
                    act.wait_ge(adj_loaded[slot(ph, c)][b // LB], loads_of_slot(k, ph, c) * 16)
                piece = marks[slot(ph, c)][:, b, :]
                nc.scalar.activation(piece, piece, ACT.Relu, scale=-BIG, bias=BIG).then_inc(marked, 1)

            def copy_d_rows(s, ph):
                act.wait_ge(d_rows_ps_ready, s + 1)
                nc.scalar.activation(d_rows[0:3, ph, :], misc_ps[0:3, :], ACT.Copy).then_inc(d_rows_ready, 1)

            def copy_w8(s, ph):
                act.wait_ge(w8_ps_ready, s + 1)
                nc.scalar.activation(w8_bcast[:, ph, :], misc_ps[:, :], ACT.Copy).then_inc(w8_ready, 1)

            def copy_h(s):
                act.wait_ge(pv_done, (s + 1) * NPAIR + CREDIT)
                act.wait_ge(sums_folded, s + 1)
                nc.scalar.activation(den_sb[:, :], den_ps[0:2 * G, :], ACT.Copy)
                nc.scalar.activation(hsum[:, :], h_ps[:, :], ACT.Copy).then_inc(h_copied, 1)

            def exp_of_h(s):
                act.wait_ge(pool_epi_step, s * NPOOL + POOL_H)
                nc.scalar.activation(y_b[:, :, :], y_a[:, :, :], ACT.Relu, scale=-1.0).then_inc(elu_exp, 1)
                act.wait_ge(elu_exp, s * 2 + 1)
                nc.scalar.activation(y_c[:, :, :], y_b[:, :, :], ACT.Exp, scale=-1.0).then_inc(elu_exp, 1)

            def period(s, k, ph, first=False, last=False):
                k1, ph1 = after(k, ph)
                for t in range(NT):
                    g = s * NT + t
                    if without_dve(t, last):
                        act.wait_ge(x_exp_ready, s * NXT + t // XP + 1)
                        exponents, bias = exp_x_ps[:, :], v2_col
                    else:
                        act.wait_ge(expo_ready, s * ND + dve_tile(t, last) + 1)
                        exponents, bias = expo[:, dve_tile(t, last) % NX, :], v_col
                    if t % 2 == 0:
                        act.wait_ge(pv_done, s * NPAIR + t // 2 + 1)
                        if t // 2 % CREDIT < GP:
                            act.wait_ge(summed, s * NGP + pair_of_gpsimd(t // 2) + 1)
                    nc.scalar.activation(probs[:, t // 2 % CREDIT, t % 2, :], exponents, ACT.Exp,
                                         bias=bias[:, t:t + 1]).then_inc(exp_done, 1)
                    if t == 2 and not first:
                        copy_h(s - 1)
                    if t == EXP_AT and not first:
                        exp_of_h(s - 1)
                    if without_dve(t + RELU_AHEAD, last) and t + RELU_AHEAD < NT:
                        nc.scalar.activation(relu_x[:, :], w8_bcast[:, ph, :], ACT.Relu,
                                             bias=v8_col[:, t + RELU_AHEAD:t + RELU_AHEAD + 1])\
                            .then_inc(relu_ready, 1)
                    if t % STEP == MARK_T and step(s, k, ph, MARK_AHEAD + t // STEP):
                        mark(*step(s, k, ph, MARK_AHEAD + t // STEP))
                    if not last:
                        if t == GUARD_AT + 1:
                            copy_d_rows(s + 1, ph1)
                        if t == GUARD_AT + 3:
                            copy_w8(s + 1, ph1)

            act.sem_inc(exp_done, FREE)
            for m in range(NT // NB):
                act.wait_ge(v_bcast_ps_ready, m + 1)
                nc.scalar.activation(v_bcast[:, m * SB:(m + 1) * SB], exp_ps[m % LEAD][:, :], ACT.Copy)\
                    .then_inc(v_bcast_ready, 1)
                if m == NT // NB - NB - 1:
                    for q in range(EARLY_MARKS):
                        mark(0, 0, q)
            for q in range(EARLY_MARKS, NQ + MARK_AHEAD):
                mark(0, q // NQ, q % NQ)
            act.wait_ge(pool_const, 10)
            copy_d_rows(0, 0)
            copy_w8(0, 0)
            superblocks(act, period)
            copy_h(NS - 1)
            exp_of_h(NS - 1)

        @block.vector
        def _(dve):
            def chained(ins, semaphore, count):
                ins.then_inc(semaphore, 1)
                dve.wait_ge(semaphore, count)

            dve.wait_ge(pool_const, 10)
            nc.vector.tensor_copy(ident_b[:, :], ident_f[:, :]).then_inc(pro_dve, 1)
            nc.vector.tensor_scalar(neg_ident[:, :], ident_f[:, :], -1.0, None, ALU.mult).then_inc(pro_dve, 1)
            dve.wait_ge(const_loaded, 48)
            for c in range(2):
                ins = nc.vector.tensor_scalar(a_wide[:, c, :], ones_f[0:F, :], a_in[:, c:c + 1], None, ALU.mult)
            ins.then_inc(pro_dve, 1)
            dve.wait_ge(pro_pe, 1)
            nc.vector.tensor_copy(wT, misc_ps[0:F, 0:F]).then_inc(pro_dve, 1)
            dve.wait_ge(pro_pe, 2)
            chained(nc.vector.tensor_copy(wa[:, :, 0, :],
                                          misc_ps[:, 128:128 + 2 * F].rearrange("p (c f) -> p c f", c=2)),
                    pro_dve, 5)
            for c in range(NC + 1):
                tiles = slice(c * CT, (c + 1) * CT)
                if c < NC:
                    dve.wait_ge(ent_loaded[c], 16)
                    chained(nc.vector.tensor_tensor(prod[:, tiles, :], ent_sb[:, tiles, :],
                                                    wa[:, 1, :, :].broadcast_to([P, CT, F]), ALU.mult),
                            v_step, 2 * c + 1)
                    nc.vector.tensor_reduce(v_col[:, tiles], prod[:, tiles, :], AX.X, ALU.add).then_inc(v_step, 1)
                if c:
                    dve.wait_ge(v_turned, c)
                    nc.vector.tensor_copy(v_rows[0:CT, c - 1, :], epi_ps[0:CT, 0, :]).then_inc(v_rows_ready, 1)
            nc.vector.tensor_scalar(v8_col[:, :], v_col[:, :], 1.0 - ALPHA, None, ALU.mult)
            nc.vector.tensor_scalar(v2_col[:, :], v_col[:, :], ALPHA, None, ALU.mult)
            nc.vector.tensor_scalar(nv8_col[:, :], v_col[:, :], -(1.0 - ALPHA), None, ALU.mult).then_inc(pro_dve, 1)
            nc.vector.tensor_tensor(fold[:, :], ident_f[:, 0:F], ident_f[:, F:2 * F], ALU.add).then_inc(pro_dve, 1)

            def w_and_mean():
                dve.wait_ge(x_prod, 2)
                nc.vector.tensor_reduce(w_col[:, :], x_all[:, :, 0:F // 2], AX.X, ALU.add).then_inc(pro_dve, 1)
                dve.wait_ge(pro_pe, 3)
                chained(nc.vector.tensor_reduce(mean_ent[:, 0, :], h_ps[:, :].rearrange("p (t f) -> p f t", f=F),
                                                AX.X, ALU.add), pro_dve, PRO_DVE)

            def row_max(ph, q, junk=junk[:, :]):
                c, b = divmod(q, NB)
                nc.vector.tensor_tensor_reduce(out=junk, in0=v_bcast[:, c * QC:(c + 1) * QC],
                                               in1=marks[slot(ph, c)][:, b, :], scale=1.0,
                                               scalar=-3.0e38, op0=ALU.subtract, op1=ALU.max,
                                               accum_out=vmax_part[:, ph, b, c:c + 1]).then_inc(maxed, 1)

            def guard(s, ph):
                n = s * NGUARD
                dve.wait_ge(maxed, (s + 1) * NQ)
                nc.vector.tensor_reduce(g_a[:, :], vmax_part[:, ph, :, :], AX.X, ALU.max).then_inc(guard_step, 1)
                chained(nc.vector.tensor_copy(w_cur[:, :], w_col[:, bass.ds(s * NB, NB)]), guard_step, n + 2)
                chained(nc.vector.tensor_tensor(g_b[:, :], g_a[:, :], w_cur[:, :], ALU.add), guard_step, n + 3)
                chained(nc.vector.scalar_tensor_tensor(out=g_a[:, :], in0=g_b[:, :], scalar=ALPHA, in1=g_b[:, :],
                                                       op0=ALU.mult, op1=ALU.max), guard_step, n + 4)
                chained(nc.vector.scalar_tensor_tensor(out=g_b[:, :], in0=w_cur[:, :], scalar=ALPHA, in1=g_a[:, :],
                                                       op0=ALU.mult, op1=ALU.subtract), guard_step, n + 5)
                chained(nc.vector.tensor_scalar(w8_cur[:, :, 0], w_cur[:, :], 1.0 - ALPHA, None, ALU.mult),
                        guard_step, n + 6)
                chained(nc.vector.tensor_copy(d_parts[:, :, 0], g_b[:, :]), guard_step, n + 7)
                chained(nc.vector.tensor_tensor(g_a[:, :], g_b[:, :], d_parts[:, :, 0], ALU.subtract),
                        guard_step, n + 8)
                chained(nc.vector.tensor_copy(d_parts[:, :, 1], g_a[:, :]), guard_step, n + 9)
                chained(nc.vector.tensor_tensor(g_c[:, :], g_a[:, :], d_parts[:, :, 1], ALU.subtract),
                        guard_step, n + 10)
                chained(nc.vector.tensor_copy(d_parts[:, :, 2], g_c[:, :]), guard_step, n + 11)

            def wide(col):
                return col.broadcast_to([P, NB, F])

            def divide(s):
                n = s * NEPI
                h, den = epi_ps[:, :, 0:F], epi_ps[:, :, F:F + 1]
                dve.wait_ge(epi_ready, (s + 1) * NB)
                if not (isinstance(s, int) and s == 0):
                    dve.wait_ge(pool_epi_step, s * NPOOL)
                chained(nc.vector.tensor_scalar(e_flag[:, :, :], den, 0.0, None, ALU.is_equal), epi_step, n + 1)
                chained(nc.vector.tensor_tensor(e_a[:, :, :], den, e_flag[:, :, :], ALU.add), epi_step, n + 2)
                chained(nc.vector.reciprocal(e_b[:, :, :], e_a[:, :, :]), epi_step, n + 3)
                nc.vector.tensor_tensor(y_a[:, :, :], h, wide(e_b[:, :, :]), ALU.mult).then_inc(epi_step, 1)

            def mean_of_y(s):
                n = s * NEPI
                dve.wait_ge(pool_epi_step, s * NPOOL + POOL_SUM)
                chained(nc.vector.tensor_reduce(e_a[:, :, 0], y_a[:, :, :], AX.X, ALU.add), epi_step, n + 5)
                nc.vector.tensor_scalar(e_b[:, :, :], e_a[:, :, :], -1.0 / F, None, ALU.mult).then_inc(epi_step, 1)

            def variance(s):
                n = s * NEPI
                dve.wait_ge(pool_epi_step, s * NPOOL + POOL_SQUARE)
                chained(nc.vector.tensor_reduce(e_b[:, :, 0], y_b[:, :, :], AX.X, ALU.add), epi_step, n + 7)
                nc.vector.tensor_scalar(e_a[:, :, :], e_b[:, :, :], 1.0 / F, EPS, ALU.mult, ALU.add)\
                    .then_inc(epi_step, 1)

            def period(s, k, ph, first=False, last=False):
                k1, ph1 = after(k, ph)
                for t in range(NT):
                    g = s * NT + t
                    if t == 0:
                        dve.wait_ge(w8_ready, s + 1)
                    n = MAX_AHEAD + t // STEP
                    maximum = step(s, k, ph, n) if t % STEP == MAX_T else None
                    if maximum:
                        dve.wait_ge(marked, (s + 1) * NQ + n + 1)
                        dve.wait_ge(maxed, (s + 1) * NQ + n)
                    if not without_dve(t, last):
                        dve.wait_ge(masked, g + 1)
                        dve.wait_ge(exp_done, g - back(t, NX, last) + 1 + FREE)
                        nc.vector.scalar_tensor_tensor(out=expo[:, dve_tile(t, last) % NX, :], in0=w8_bcast[:, ph, :],
                                                       scalar=nv8_col[:, t:t + 1],
                                                       in1=exp_ps[dve_tile(t, last) % LEAD][:, :],
                                                       op0=ALU.max, op1=ALU.add).then_inc(expo_ready, 1)
                    if maximum:
                        row_max(*maximum[1:])
                    if not first:
                        if t == DIVIDE_AT:
                            divide(s - 1)
                        if t == MEAN_AT:
                            mean_of_y(s - 1)
                        if t == VARIANCE_AT:
                            variance(s - 1)
                    if not last and t == GUARD_AT:
                        guard(s + 1, ph1)

            for n in range(NQ + MAX_AHEAD):
                if n % NB == 0 and n < NQ:
                    dve.wait_ge(v_bcast_ready, n + NB)
                dve.wait_ge(marked, n + 1)
                if n >= 2:
                    dve.wait_ge(maxed, n - 1)
                row_max(n // NQ, n % NQ, early_junk[n % 2])
                if n == NQ - 2:
                    w_and_mean()
                if n == NQ - 1:
                    guard(0, 0)
            superblocks(dve, period)
            divide(NS - 1)
            mean_of_y(NS - 1)
            variance(NS - 1)

        @block.tensor
        def _(pe):
            def broadcast_v(c):
                for t in range(CT):
                    m = (c * CT + t) // NB
                    if t % NB == 0 and m >= LEAD:
                        pe.wait_ge(v_bcast_ready, m - LEAD + 1)
                    mm = nc.tensor.matmul(exp_ps[m % LEAD][:, t % NB * P:(t % NB + 1) * P],
                                          ident_f[:, t:t + 1].broadcast_to([P, P]), v_rows[:, c, :],
                                          start=True, stop=True)
                    if t % NB == NB - 1:
                        mm.then_inc(v_bcast_ps_ready, 1)

            pe.wait_ge(pool_const, 10)
            pe.wait_ge(const_loaded, 48)
            nc.tensor.matmul(misc_ps[0:F, 0:F], w_in, ident_f[0:F, 0:F], start=True, stop=True).then_inc(pro_pe, 1)
            pe.wait_ge(pro_dve, 4)
            for c in range(2):
                mm = nc.tensor.matmul(misc_ps[:, 128 + c * F:128 + (c + 1) * F], a_wide[:, c, :], wT,
                                      start=True, stop=True)
            mm.then_inc(pro_pe, 1)
            for c in range(NC):
                pe.wait_ge(v_step, 2 * (c + 1))
                if c:
                    pe.wait_ge(v_rows_ready, c)
                nc.tensor.matmul(epi_ps[0:CT, 0, :], v_col[:, c * CT:(c + 1) * CT], ident_f[:, :],
                                 start=True, stop=True).then_inc(v_turned, 1)
                if c:
                    broadcast_v(c - 1)
            pe.wait_ge(v_rows_ready, NC)
            broadcast_v(NC - 1)
            for t in range(0, NT, SB // F):
                mm = nc.tensor.matmul(h_ps[:, :], mean_w, ent_sb[:, t:t + SB // F, :], start=(t == 0),
                                      stop=(t + SB // F == NT))
            mm.then_inc(pro_pe, 1)

            def mask(s, ph, t, wait=True, last=False):
                if without_dve(t, last):
                    if wait and not (isinstance(s, int) and s == 0 and t < XP):
                        pe.wait_ge(exp_done, s * NT + t - XP + 1 + FREE)
                elif wait:
                    pe.wait_ge(expo_ready, s * ND + dve_tile(t, last) - LEAD + 1)
                if t == 0:
                    pe.wait_ge(d_rows_ready, s + 1)
                bank = exp_x_ps if without_dve(t, last) else exp_ps[dve_tile(t, last) % LEAD]
                nc.tensor.matmul(bank[:, :], ones_b[:, :], d_rows[:, ph, :], start=True, stop=True,
                                 skip_group_check=True)
                for b in range(NB):
                    mm = nc.tensor.matmul(bank[:, b * P:(b + 1) * P],
                                          marks[slot(ph, t // CT)][:, b, t % CT * P:(t % CT + 1) * P],
                                          neg_ident[:, :], start=False, stop=True,
                                          skip_group_check=True)
                mm.then_inc(masked, 1)

            def add_relu(s, t):
                pe.wait_ge(relu_ready, s * NXT + t // XP + 1)
                nc.tensor.matmul(exp_x_ps[:, :], ident_f[:, :], relu_x[:, :], start=False, stop=True,
                                 skip_group_check=True).then_inc(x_exp_ready, 1)

            def weighted(s, pair):
                pe.wait_ge(exp_done, (s * NPAIR + pair + 1) * 2 + FREE)
                for i in range(2):
                    mm = nc.tensor.matmul(h_ps[i * F:(i + 1) * F, :], ent_sb[:, 2 * pair + i, :],
                                          probs[:, pair % CREDIT, i, :], start=(pair == 0), stop=(pair == NPAIR - 1),
                                          skip_group_check=True)
                if pair % CREDIT >= GP:
                    for i in range(2):
                        mm = nc.tensor.matmul(den_ps[i * G:(i + 1) * G, :], ones_f[:, 0:G],
                                              probs[:, pair % CREDIT, i, :], start=(pair == GP),
                                              stop=False, skip_group_check=True)
                mm.then_inc(pv_done, 1)

            def guard_rows(s):
                pe.wait_ge(guard_step, s * NGUARD + 11)
                if not (isinstance(s, int) and s == 0):
                    pe.wait_ge(w8_ready, s)
                for b in range(NB):
                    mm = nc.tensor.matmul(misc_ps[0:3, b * P:(b + 1) * P], d_parts[:, b, :], ident_b[:, :],
                                          start=True, stop=True)
                mm.then_inc(d_rows_ps_ready, 1)

            def guard_w8(s):
                pe.wait_ge(d_rows_ready, s + 1)
                pe.wait_ge(w8_diag_ready, s + 1)
                nc.tensor.matmul(misc_ps[:, :], ones_f[:, :], w8_diag[:, :], start=True, stop=True)\
                    .then_inc(w8_ps_ready, 1)

            def fold_sums(s):
                pe.wait_ge(summed, (s + 1) * NGP + GP)
                for i in range(2):
                    mm = nc.tensor.matmul(den_ps[i * G:(i + 1) * G, :], ones_f[:, 0:G], dsum[:, i, :],
                                          start=False, stop=True, skip_group_check=True)
                mm.then_inc(sums_folded, 1)

            def turn(s, b):
                if b == 0:
                    pe.wait_ge(h_copied, s + 1)
                    if not (isinstance(s, int) and s == 0):
                        pe.wait_ge(epi_step, s * NEPI)
                nc.tensor.matmul(epi_ps[:, b, 0:F], hsum[:, b * P:(b + 1) * P], fold[:, :], start=True, stop=True)
                nc.tensor.matmul(epi_ps[:, b, F:F + 1], den_sb[:, b * P:(b + 1) * P], per_g[:, :],
                                 start=True, stop=True).then_inc(epi_ready, 1)

            def period(s, k, ph, first=False, last=False):
                k1, ph1 = after(k, ph)
                for t in range(NT):
                    if t + LEAD < NT:
                        mask(s, ph, t + LEAD, last=last)
                    elif not last:
                        mask(s + 1, ph1, t + LEAD - NT)
                    if t == 1 and not first:
                        weighted(s - 1, NPAIR - 1)
                        fold_sums(s - 1)
                    if t % 2 == 1 and t > 1:
                        if t == 3 and not first:
                            pe.wait_ge(h_copied, s)
                        weighted(s, t // 2 - 1)
                    if without_dve(t + ADD_AHEAD, last) and t + ADD_AHEAD < NT:
                        add_relu(s, t + ADD_AHEAD)
                    if not first and t in TURN_AT:
                        turn(s - 1, TURN_AT.index(t))
                    if not last and t == GUARD_AT + 1:
                        guard_rows(s + 1)
                    if not last and t == GUARD_AT + 2:
                        guard_w8(s + 1)

            pe.sem_inc(pv_done, CREDIT)
            pe.wait_ge(pro_dve, PRO_DVE)
            guard_rows(0)
            guard_w8(0)
            pe.wait_ge(v_bcast_ready, NT // NB)
            for t in range(LEAD):
                mask(0, 0, t, wait=False)
            superblocks(pe, period)
            weighted(NS - 1, NPAIR - 1)
            fold_sums(NS - 1)
            for b in range(NB):
                turn(NS - 1, b)


_INS = ["x", "adj", "L0_gnn_entity_embs", "L0_gnn_W", "L0_gnn_a"]


def kernel(**inputs):
    import numpy as _np
    import concourse.bacc as _bacc
    from concourse import mybir as _mybir
    from concourse.bass_utils import run_bass_kernel_spmd as _run

    nc = _bacc.Bacc("TRN2", target_bir_lowering=False, num_devices=1)
    arrays, args = {}, []
    for name in _INS:
        a = _np.ascontiguousarray(inputs[name])
        arrays[f"in_{name}_dram"] = a
        args.append(nc.dram_tensor(f"in_{name}_dram", a.shape, _mybir.dt.from_np(a.dtype), kind="ExternalInput").ap())
    shape = tuple(inputs["x"].shape)
    out = nc.dram_tensor("out_0_dram", shape, _mybir.dt.float32, kind="ExternalOutput").ap()
    gat_resnorm_kernel(nc, *args, out)
    r = _run(nc, [arrays], core_ids=[0])
    return r.results[0]["out_0_dram"]
```
